# Optimizing a Trainium2 kernel written in Bass

```python
import numpy as np
import jax
import jax.numpy as jnp

def _softmax(x, axis=-1):
    return jax.nn.softmax(x, axis=axis)

def _gelu(x):
    return jax.nn.gelu(x, approximate=True)

def _silu(x):
    return jax.nn.silu(x)

def _sigmoid(x):
    return jax.nn.sigmoid(x)

def _layernorm(x, axis=-1, eps=1e-05):
    m = jnp.mean(x, axis=axis, keepdims=True)
    v = jnp.var(x, axis=axis, keepdims=True)
    return (x - m) / jnp.sqrt(v + eps)

def _scatter_add(tgt, idx, src, axis=0):
    return tgt.at[idx].add(src)

def _segment_sum(src, seg, n):
    return jax.ops.segment_sum(src, seg, n)
kernel_name = 'mk_cond_seq_d1_seqx_r4_e648ad'

def setup_inputs(seed: int=0):
    np.random.seed(seed)
    _w = jnp.asarray

    def _rec_inputs():
        import jax
        import jax.numpy as jnp
        _rk = jax.random.key(seed)
        x = 1.648e-05 + 1 * jax.random.normal(jax.random.fold_in(_rk, 1), (4, 512, 288), jnp.float32)
        _lenS = 512 - jax.random.randint(jax.random.fold_in(_rk, 7), (4,), 0, max(1, 512 // 4) + 1, jnp.int32)
        _lenS2 = 512 - jax.random.randint(jax.random.fold_in(_rk, 8), (4,), 0, max(1, 512 // 4) + 1, jnp.int32)
        cond_1152 = 0.00914911 + 1.00357 * jax.random.normal(jax.random.fold_in(_rk, 11), (4, 288), jnp.float32)
        return (x, cond_1152)
    x, cond_1152 = _rec_inputs()

    def _L0_cond_setup():
        import jax, jax.numpy as jnp
        import numpy as np
        B, L, C = (8, 256, 288)
        H = 16
        D = C // H
        FF = int(C * 4.0)
        EPS = 1e-06

        def _layernorm(x):
            mu = jnp.mean(x, axis=-1, keepdims=True)
            var = jnp.mean(jnp.square(x - mu), axis=-1, keepdims=True)
            return (x - mu) * jax.lax.rsqrt(var + EPS)

        def _modulate(x, shift, scale):
            return x * (1.0 + scale) + shift

        def _attention(h, W_qkv, b_qkv, W_proj, b_proj):
            b, l, c = h.shape
            qkv = h @ W_qkv + b_qkv
            qkv = qkv.reshape(b, l, 3, H, D)
            q, k, v = (qkv[:, :, 0], qkv[:, :, 1], qkv[:, :, 2])
            scale = D ** (-0.5)
            scores = jnp.einsum('blhd,bmhd->bhlm', q * scale, k)
            attn = jax.nn.softmax(scores, axis=-1)
            o = jnp.einsum('bhlm,bmhd->blhd', attn, v).reshape(b, l, c)
            return o @ W_proj + b_proj
        key = jax.random.key(seed)
        ks = jax.random.split(key, 12)
        s = 0.02
        return {'x': jax.random.normal(ks[0], (B, L, C), jnp.float32), 'c': jax.random.normal(ks[1], (B, 1, C), jnp.float32), 'W_qkv': jax.random.normal(ks[2], (C, 3 * C), jnp.float32) * s, 'b_qkv': jnp.zeros((3 * C,), jnp.float32), 'W_proj': jax.random.normal(ks[3], (C, C), jnp.float32) * s, 'b_proj': jnp.zeros((C,), jnp.float32), 'W_fc1': jax.random.normal(ks[4], (C, FF), jnp.float32) * s, 'b_fc1': jnp.zeros((FF,), jnp.float32), 'W_fc2': jax.random.normal(ks[5], (FF, C), jnp.float32) * s, 'b_fc2': jnp.zeros((C,), jnp.float32), 'W_ada': jax.random.normal(ks[6], (C, 6 * C), jnp.float32) * s, 'b_ada': jnp.zeros((6 * C,), jnp.float32)}
    _L0_cond_all = _L0_cond_setup()
    _L0_cond_in = {k: v for k, v in _L0_cond_all.items() if k in ('W_qkv', 'b_qkv', 'W_proj', 'b_proj', 'W_fc1', 'b_fc1', 'W_fc2', 'b_fc2', 'W_ada', 'b_ada')}
    del _L0_cond_all
    return {'x': x, 'cond_1152': cond_1152, 'L0_cond_W_qkv': _L0_cond_in['W_qkv'], 'L0_cond_b_qkv': _L0_cond_in['b_qkv'], 'L0_cond_W_proj': _L0_cond_in['W_proj'], 'L0_cond_b_proj': _L0_cond_in['b_proj'], 'L0_cond_W_fc1': _L0_cond_in['W_fc1'], 'L0_cond_b_fc1': _L0_cond_in['b_fc1'], 'L0_cond_W_fc2': _L0_cond_in['W_fc2'], 'L0_cond_b_fc2': _L0_cond_in['b_fc2'], 'L0_cond_W_ada': _L0_cond_in['W_ada'], 'L0_cond_b_ada': _L0_cond_in['b_ada']}

def reference(x, cond_1152, L0_cond_W_qkv, L0_cond_b_qkv, L0_cond_W_proj, L0_cond_b_proj, L0_cond_W_fc1, L0_cond_b_fc1, L0_cond_W_fc2, L0_cond_b_fc2, L0_cond_W_ada, L0_cond_b_ada):
    import jax
    import jax.numpy as jnp

    def _L0_cond_ref(x, c, W_qkv, b_qkv, W_proj, b_proj, W_fc1, b_fc1, W_fc2, b_fc2, W_ada, b_ada):
        import jax, jax.numpy as jnp
        import numpy as np
        B, L, C = (8, 256, 288)
        H = 16
        D = C // H
        FF = int(C * 4.0)
        EPS = 1e-06

        def _layernorm(x):
            mu = jnp.mean(x, axis=-1, keepdims=True)
            var = jnp.mean(jnp.square(x - mu), axis=-1, keepdims=True)
            return (x - mu) * jax.lax.rsqrt(var + EPS)

        def _modulate(x, shift, scale):
            return x * (1.0 + scale) + shift

        def _attention(h, W_qkv, b_qkv, W_proj, b_proj):
            b, l, c = h.shape
            qkv = h @ W_qkv + b_qkv
            qkv = qkv.reshape(b, l, 3, H, D)
            q, k, v = (qkv[:, :, 0], qkv[:, :, 1], qkv[:, :, 2])
            scale = D ** (-0.5)
            scores = jnp.einsum('blhd,bmhd->bhlm', q * scale, k)
            attn = jax.nn.softmax(scores, axis=-1)
            o = jnp.einsum('bhlm,bmhd->blhd', attn, v).reshape(b, l, c)
            return o @ W_proj + b_proj
        ada = jax.nn.silu(c) @ W_ada + b_ada
        shift_msa, scale_msa, gate_msa, shift_mlp, scale_mlp, gate_mlp = jnp.split(ada, 6, axis=-1)
        h = _modulate(_layernorm(x), shift_msa, scale_msa)
        x = x + gate_msa * _attention(h, W_qkv, b_qkv, W_proj, b_proj)
        h = _modulate(_layernorm(x), shift_mlp, scale_mlp)
        mlp = jax.nn.gelu(h @ W_fc1 + b_fc1, approximate=True) @ W_fc2 + b_fc2
        x = x + gate_mlp * mlp
        return x
    x = _L0_cond_ref(x, cond_1152[:, None, :], L0_cond_W_qkv, L0_cond_b_qkv, L0_cond_W_proj, L0_cond_b_proj, L0_cond_W_fc1, L0_cond_b_fc1, L0_cond_W_fc2, L0_cond_b_fc2, L0_cond_W_ada, L0_cond_b_ada)
    return x

_drawn_inputs = setup_inputs


def setup_inputs(seed=0):
    import zlib

    import numpy as np

    out = dict(_drawn_inputs(seed))
    spreads = {'L0_cond_b_qkv': (0.0, 0.8),
     'L0_cond_b_proj': (0.0, 0.366),
     'L0_cond_b_fc1': (0.0, 0.8),
     'L0_cond_b_fc2': (0.0, 0.361),
     'L0_cond_b_ada': (0.0, 0.393)}
    factors = {'L0_cond_W_qkv': 8.0, 'L0_cond_W_proj': 5.476}
    for name, (base, spread) in spreads.items():
        noise = np.random.default_rng([zlib.crc32(name.encode()), seed]).standard_normal(out[name].shape)
        drawn = base * np.exp(spread * noise) if base else spread * noise
        out[name] = jnp.asarray(drawn.astype(out[name].dtype))
    for name, factor in factors.items():
        out[name] = (out[name] * factor).astype(out[name].dtype)
    return out
```

```python
import concourse.bass as bass
from concourse import mybir
from contextlib import ExitStack

B, L, C = 4, 512, 288
H = 16
D = C // H
FF = 4 * C
EPS = 1e-6
SCALE = float(D) ** -0.5
P = 128
TT = L // P
KC = C // P
REM = C - KC * P
assert 4 * REM == P
G = 4
NG = H // G
SLOTS = P // D
QKT = -(-2 * H // SLOTS)
QROWS = 6 * D
MROW = QROWS
FM = FF // P
U = 2 * TT
N1 = G * TT


def qk_rows(m):
    return min(SLOTS, 2 * H - m * SLOTS) * D


def build(nc, x, cond, w_qkv, b_qkv, w_proj, b_proj, w_fc1, b_fc1, w_fc2, b_fc2, w_ada, b_ada, out):
    f32, f32r, bf16 = mybir.dt.float32, mybir.dt.float32r, mybir.dt.bfloat16
    ALU = mybir.AluOpType
    ACT = mybir.ActivationFunctionType
    AX = mybir.AxisListType.X

    ctx = ExitStack()
    with ctx:
        def sb(name, shape, dt):
            return ctx.enter_context(nc.sbuf_tensor(name, shape, dt))

        def sem(name):
            return ctx.enter_context(nc.semaphore(name))

        WqH, WqL, WqR = sb("WqH", [P, KC, 3 * C], f32r), sb("WqL", [P, KC, 3 * C], f32r), sb("WqR", [P, 3 * C], f32r)
        W1H, W1L, W1R = sb("W1H", [P, KC, FF], f32r), sb("W1L", [P, KC, FF], f32r), sb("W1R", [P, FF], f32r)
        W2H, W2L = sb("W2H", [P, FM, C], f32r), sb("W2L", [P, FM, C], f32r)
        WpH, WpL = sb("WpH", [P, NG, C], f32r), sb("WpL", [P, NG, C], f32r)
        QS, KS = sb("QS", [P, H, L], bf16), sb("KS", [P, H, L], bf16)
        Pr = sb("Pr", [P, 4, 2, L], f32)
        V = sb("V", [P, TT, H, 32], f32)
        qk3 = sb("qk3", [P, 2, 3, L], bf16)
        FT = sb("FT", [P, 3, L], f32)
        FQ = sb("FQ", [P, 2, L], f32)
        rnd = sb("rnd", [P, L], f32r)
        hAH, hAL, hAR = sb("hAH", [P, KC, L], f32r), sb("hAL", [P, KC, L], f32r), sb("hAR", [P, L], f32r)
        hMH, hML, hMR = sb("hMH", [P, KC, L], f32r), sb("hML", [P, KC, L], f32r), sb("hMR", [P, L], f32r)
        oH, oL = sb("oH", [P, NG, L], f32r), sb("oL", [P, NG, L], f32r)
        oS = sb("oS", [P, L], f32)
        xs = sb("xs", [P, TT, 3 * P], f32)
        x1 = sb("x1", [P, TT, C], f32)
        tmp = sb("tmp", [P, 2, C], f32)
        gate = sb("gate", [P, 2, C], f32)
        gb = sb("gb", [P, 2, C], f32)
        biasB = sb("biasB", [P, 3, C], f32)
        ident = sb("ident", [P, P], f32)
        selden = sb("selden", [P, G], f32)
        mask = sb("mask", [P, 2], f32)
        biasC = sb("biasC", [P, 26], f32)
        ada = sb("ada", [P, 12, B], f32)
        cT = sb("cT", [96, 3, B], f32)
        st, mv, rs, half = sb("st", [P, TT, 6], f32), sb("mv", [P, 4, TT], f32), sb("rs", [P, 2, TT], f32), sb("half", [P, TT], f32)
        mean, var = sb("mean", [P, TT], f32), sb("var", [P, TT], f32)
        epsT, ve, seed = sb("epsT", [P, TT], f32), sb("ve", [P, TT], f32), sb("seed", [P, 4], f32)
        mx = sb("mx", [P, 2, N1], f32)
        rec = sb("rec", [P, N1], f32)
        mr = sb("mr", [16, 2, 3, P], bf16)
        mres = sb("mres", [16, P], f32)
        cS, cA = FT[0:B, 0, 0:C], FT[0:B, 1, 0:C]
        rows, rem4, rem4x = FQ[0:22, 0, 0:P], FQ[0:4, 1, 0:REM], FQ[0:4, 1, P:2 * P]
        recx = tmp[:, :, :].rearrange("p a b -> p (a b)")[:, 0:L]
        gateS = x1[0:B, 0:2, :]
        PrF = Pr[:, :, :, :].rearrange("p a b c -> p (a b c)")
        WaC = PrF[0:96, 0:12 * C].rearrange("p (k v n) -> p k v n", k=3, v=4)
        WaG = PrF[0:96, 0:6 * C].rearrange("p (k v n) -> p k v n", k=3, v=2)
        W1S = PrF[:, 0:3 * FF].rearrange("p (k n) -> p k n", k=3)
        WqS = V[:, :, :, :].rearrange("p a b c -> p (a b c)")[:, 0:2 * 3 * C].rearrange("p (k n) -> p k n", k=2)
        X1S = x1[:, :, :].rearrange("p a b -> p (a b)")

        scr = nc.dram_tensor("qk_scratch", (3, 2 * H * D, L), bf16, kind="Internal").ap()
        gscr = nc.dram_tensor("gate_scratch", (B, 2, C), f32, kind="Internal").ap()

        A = [ctx.enter_context(nc.psum_tensor(f"A{i}", [P, L], f32)) for i in range(2)]
        BB = [ctx.enter_context(nc.psum_tensor(f"B{i}", [P, 2, L], f32)) for i in range(2)]
        Cb = ctx.enter_context(nc.psum_tensor("Cb", [P, L], f32))
        Db = ctx.enter_context(nc.psum_tensor("Db", [P, L], f32))
        CD = [Cb, Db]

        d_x, d_x1, d_gate = sem("d_x"), sem("d_x1"), sem("d_gate")
        d_c, d_bias, d_bb, d_bgate, d_wac, d_wag, d_wq, d_wqr, d_w1, d_stage, d_gs = (sem(n) for n in (
            "d_c", "d_bias", "d_bb", "d_bgate", "d_wac", "d_wag", "d_wq", "d_wqr", "d_w1", "d_stage", "d_gs"))
        d_scr = [sem(f"d_scr{i}") for i in range(2)]
        d_stk = [sem(f"d_stk{i}") for i in range(NG)]
        d_mrow = [sem(f"d_mrow{i}") for i in range(2)]
        d_out = sem("d_out")
        pe_c, pe_bias, pe_ada, pe_gate = sem("pe_c"), sem("pe_bias"), sem("pe_ada"), sem("pe_gate")
        t1, qk, vv, p1, mt, p2, av, den, rct, pj, t2, f1, f2 = (sem(n) for n in (
            "t1", "qk", "vv", "p1", "mt", "p2", "av", "den", "rct", "pj", "t2", "f1", "f2"))
        a_silu, t1f, t2f, qkf, ex, osd, gl = (sem(n) for n in ("a_silu", "t1f", "t2f", "qkf", "ex", "osd", "gl"))
        v_init, v_c, v_bias, v_ada, v_gate, v_wq, v_wst = (sem(n) for n in (
            "v_init", "v_c", "v_bias", "v_ada", "v_gate", "v_wq", "v_wst"))
        ln1s, ln1v, ln2s, ln2v, xn1, xn2 = (sem(n) for n in ("ln1s", "ln1v", "ln2s", "ln2v", "xn1", "xn2"))
        h1h, h1r, h2h, h2r, q2, vf, mxd, mread, mstep, rc, om, onh, pjt, pjx, gh, gs, yt, yd = (sem(n) for n in (
            "h1h", "h1r", "h2h", "h2r", "q2", "vf", "mxd", "mread", "mstep", "rc", "om", "onh", "pjt", "pjx",
            "gh", "gs", "yt", "yd"))
        g_init, g_rs1, g_rs2, h1l, h2l, qr, q3, onl, g_gb, g_x1, g_x2, g_w = (sem(n) for n in (
            "g_init", "g_rs1", "g_rs2", "h1l", "h2l", "qr", "q3", "onl", "g_gb", "g_x1", "g_x2", "g_w"))
        g_ve = [sem("g_ve1"), sem("g_ve2")]
        g_x0, rinv, xnr, ln1a, ln2a = sem("g_x0"), sem("rinv"), [sem("xnr1"), sem("xnr2")], sem("ln1a"), sem("ln2a")

        block = ctx.enter_context(nc.Block())

        PRE = 6
        STAGED = [(WpH[:, :, :], WpL[:, :, :], NG), (W2H[:, 0:4, :], W2L[:, 0:4, :], 4),
                  (W2H[:, 4:8, :], W2L[:, 4:8, :], 4), (W2H[:, 8:9, :], W2L[:, 8:9, :], 1)]
        STAGED_AT = [16 * (G + r) for r in range(4)]
        REST = [(0, n) for n in range(PRE, N1)] + [(1, n) for n in range(N1)]
        MLP_P1 = [REST[3 * m:3 * m + 3] for m in range(FM)]

        def load_gate(sp, b):
            sp.dma_start(gate[:, :, :], gscr[b].partition_broadcast(P)).then_inc(d_gate, 16)

        def load_x1(sp, b):
            sp.dma_start(x1[:, :, :], x[b].rearrange("(t p) c -> p t c", p=P)).then_inc(d_x1, 16)

        def mrow(sp, b, g):
            sp.wait_ge(mstep, 3 * (NG * b + g + 1))
            for j in range(3):
                sp.dma_start(QS[MROW + j:MROW + j + 1, g * G:(g + 1) * G, :], mr[:, g % 2, j, :]).then_inc(d_mrow[g % 2], 16)

        def front(sp, b):
            for m in range(QKT):
                sp.wait_ge(q3, QKT * b + m + 1)
                r, n = m * SLOTS * D, qk_rows(m)
                sp.dma_start(scr[:, r:r + n, :].rearrange("j r t -> r j t"), qk3[0:n, m % 2, :, :]).then_inc(d_scr[m % 2], 16)
            if not (isinstance(b, int) and b == 0):
                sp.wait_ge(p2, U * (NG * (b - 1) + 1))
            sp.wait_ge(d_scr[0], 48 * b + 48)
            sp.wait_ge(d_scr[1], 32 * b + 32)
            for g in range(NG):
                stacks(sp, b, g)

        def stacks(sp, b, g):
            q0, k0 = g * G * D, (H + g * G) * D

            def part(j, r0):
                return scr[j, r0:r0 + G * D, :].rearrange("(h r) t -> r h t", r=D)

            hs = slice(g * G, (g + 1) * G)
            if g > 0 and not (isinstance(b, int) and b == 0):
                sp.wait_ge(p2, U * (NG * (b - 1) + g + 1))
            for i, (j, k) in enumerate(((0, 0), (0, 1), (0, 2), (1, 0), (1, 1), (2, 0))):
                sp.dma_start(QS[i * D:(i + 1) * D, hs, :], part(j, q0)).then_inc(d_stk[g], 16)
                sp.dma_start(KS[i * D:(i + 1) * D, hs, :], part(k, k0)).then_inc(d_stk[g], 16)

        def body(sp, b, more):
            mrow(sp, b, 1)
            if more:
                sp.wait_ge(yd, TT * b + 1)
                sp.wait_ge(t1, 3 * b + 3)
                sp.wait_ge(v_init, 2)
                sp.dma_start(xs[:, :, 0:C], x[b + 1].rearrange("(t p) c -> p t c", p=P)).then_inc(d_x, 16)
            for g in (2, 3):
                mrow(sp, b, g)
            if more:
                front(sp, b + 1)
                mrow(sp, b + 1, 0)
            for t in range(TT):
                sp.wait_ge(yd, TT * b + t + 2)
                sp.wait_ge(v_init, 2)
                sp.dma_start(out[b, t * P:(t + 1) * P, :], x1[:, t, :]).then_inc(d_out, 16)
            if more:
                load_gate(sp, b + 1)
                sp.wait_ge(d_out, 16 * TT * (b + 1))
                sp.wait_ge(v_init, 2)
                load_x1(sp, b + 1)

        @block.sync
        def _(sp):
            sp.dma_start(xs[:, :, 0:C], x[0].rearrange("(t p) c -> p t c", p=P)).then_inc(d_x, 16)
            sp.dma_start(cS, cond).then_inc(d_c, 16)
            wa = w_ada.rearrange("(k p) (s n) -> p k s n", p=96, n=C)
            for k in range(3):
                sp.dma_start(WaC[:, k, 0:2, :], wa[:, k, 0:2, :]).then_inc(d_wac, 16)
                sp.dma_start(WaC[:, k, 2:4, :], wa[:, k, 3:5, :]).then_inc(d_wac, 16)
            sp.wait_ge(v_init, 1)
            sp.dma_start(FQ[0:FM, 0, 0:P], b_fc1.rearrange("(m p) -> m p", p=P)).then_inc(d_bias, 16)
            n = (2 * C) // (SLOTS * D)
            sp.dma_start(FQ[FM:FM + n, 0, 0:SLOTS * D], b_qkv[0:n * SLOTS * D].rearrange("(m p) -> m p", m=n)).then_inc(d_bias, 16)
            sp.dma_start(FQ[FM + n:FM + n + 1, 0, 0:2 * C - n * SLOTS * D],
                         b_qkv[n * SLOTS * D:2 * C].rearrange("(o p) -> o p", o=1)).then_inc(d_bias, 16)
            for v, s in enumerate((0, 1, 3, 4)):
                r = FM + QKT + 2 * v
                sp.dma_start(FQ[r:r + 2, 0, 0:P], b_ada[s * C:s * C + 2 * P].rearrange("(c p) -> c p", p=P)).then_inc(d_bias, 16)
                sp.dma_start(FQ[v:v + 1, 1, 0:REM],
                             b_ada[s * C + 2 * P:(s + 1) * C].rearrange("(o p) -> o p", o=1)).then_inc(d_bias, 16)
            wq = w_qkv[0:KC * P, :].rearrange("(k p) n -> p k n", p=P)
            for k in range(KC):
                sp.dma_start(WqS[:, k, :], wq[:, k, :]).then_inc(d_wq, 16)
            for q in range(4):
                sp.dma_start(X1S[q * REM:(q + 1) * REM, 0:3 * C], w_qkv[KC * P:C, :]).then_inc(d_wqr, 16)
            for i, v in enumerate((b_proj[:], b_fc2[:], b_qkv[2 * C:3 * C])):
                sp.dma_start(biasB[:, i, :], v.partition_broadcast(P)).then_inc(d_bb, 16)
            for i, s in enumerate((2, 5)):
                sp.dma_start(tmp[0:B, i, :], b_ada[s * C:(s + 1) * C].partition_broadcast(B)).then_inc(d_bgate, 16)
            sp.wait_ge(pe_ada, 1)
            for k in range(3):
                for v, s in enumerate((2, 5)):
                    sp.dma_start(WaG[:, k, v, :], wa[:, k, s, :]).then_inc(d_wag, 16)
            sp.wait_ge(v_init, 2)
            front(sp, 0)
            sp.wait_ge(v_gate, 1)
            sp.dma_start(gscr[:, :, :], gateS).then_inc(d_gs, 16)
            w1 = w_fc1[0:KC * P, :].rearrange("(k p) n -> p k n", p=P)
            for k in range(KC):
                sp.dma_start(W1S[:, k, :], w1[:, k, :]).then_inc(d_w1, 16)
            for q in range(4):
                sp.dma_start(W1S[q * REM:(q + 1) * REM, KC, :], w_fc1[KC * P:C, :]).then_inc(d_w1, 16)
            sp.wait_ge(d_gs, 16)
            load_gate(sp, 0)
            mrow(sp, 0, 0)
            sp.wait_ge(g_w, 5)
            load_x1(sp, 0)
            with sp.Fori(0, B - 1) as b:
                body(sp, b, True)
            body(sp, B - 1, False)
            sp.wait_ge(d_out, 16 * TT * B)

        def three(o, groups, N, tail=None):
            i, first = None, True
            for (lh, ll, rh, rl) in groups:
                for a, c in ((lh, rh), (lh, rl), (ll, rh)):
                    last = tail is None and a is ll and lh is groups[-1][0]
                    i = nc.tensor.matmul(o, a, c, start=first, stop=last)
                    first = False
            if tail is not None:
                i = nc.tensor.matmul(o, tail[0], tail[1], start=False, stop=True)
            return i

        def t_front(b):
            pe = nc.tensor
            pe.wait_ge(xn1, TT * (b + 1))
            for c in range(3):
                t_chunk(c, b, t1, t1f)

        def t_chunk(c, b, done, read):
            pe = nc.tensor
            if c == 2:
                pe.wait_ge(read, 3 * b + 2)
            for t in range(TT):
                i = pe.transpose(A[c % 2][:, t * P:(t + 1) * P], xs[:, t, c * P:(c + 1) * P], ident[:, :])
            i.then_inc(done, 1)

        def qk_front(b):
            for m in range(QKT):
                qk_tile(b, m)

        def qk_tile(b, m):
            pe = nc.tensor
            if m == 0:
                pe.wait_ge(h1r, 2 * b + 2)
                pe.wait_ge(h1h, 2 * b + 2)
                pe.wait_ge(h1l, 2 * b + 2)
                pe.wait_ge(v_wq, 4)
                pe.wait_ge(t1f, 3 * b + 3)
            if m >= 2:
                pe.wait_ge(qkf, 2 * (QKT * b + m - 1))
            r, n = m * SLOTS * D, qk_rows(m)
            three(A[(m + 1) % 2][0:n, :],
                  [(WqH[:, k, r:r + n], WqL[:, k, r:r + n], hAH[:, k, :], hAL[:, k, :]) for k in range(KC)],
                  L, (WqR[:, r:r + n], hAR[:, :])).then_inc(qk, 1)

        def v_front(b, t):
            pe = nc.tensor
            if t < 2:
                pe.wait_ge(qkf, 2 * (QKT * b + QKT - 1 + t))
            else:
                pe.wait_ge(vf, TT * b + t - 1)
            ts, n = slice(t * P, (t + 1) * P), slice(2 * C, 3 * C)
            three(A[t % 2][:, 0:C],
                  [(hAH[:, k, ts], hAL[:, k, ts], WqH[:, k, n], WqL[:, k, n]) for k in range(KC)],
                  C, (hAR[:, ts], WqR[:, n])).then_inc(vv, 1)

        def row_max(b, g, n):
            pe = nc.tensor
            h, qb = g * G + n // TT, n % TT
            if n == 0:
                pe.wait_ge(d_stk[g], 192 * (b + 1))
            if n >= 2:
                pe.wait_ge(mxd, N1 * (NG * b + g) + n - 1)
            elif g == 0:
                pe.wait_ge(vf, TT * b + 3 + n)
            else:
                pe.wait_ge(mxd, N1 * (NG * b + g))
                if g == 2:
                    pe.wait_ge(t2f, 3 * b + 1)
            pe.matmul(A[n % 2][:, :], QS[0:QROWS, h, qb * P:(qb + 1) * P], KS[0:QROWS, h, :],
                      start=True, stop=True).then_inc(p1, 1)

        def max_rows(b, g):
            nc.tensor.wait_ge(mxd, N1 * (NG * b + g + 1))
            nc.tensor.transpose(Db[0:N1, 0:P], mx[:, g % 2, :], ident[:, :]).then_inc(mt, 1)

        def scores(b, g, u):
            pe = nc.tensor
            kb, hp = u // 2, u % 2
            if u == 0:
                pe.wait_ge(d_mrow[g % 2], 48 * (2 * b + g // 2 + 1))
            if g == 0 and u < 2:
                pe.wait_ge(yd, TT * b + 1)
            else:
                pe.wait_ge(ex, U * (NG * b + g) + u - 1)
            for j in range(2):
                h = g * G + 2 * hp + j
                i = pe.matmul(BB[u % 2][:, j, :], KS[0:MROW + 3, h, kb * P:(kb + 1) * P], QS[0:MROW + 3, h, :],
                              start=True, stop=True)
            i.then_inc(p2, 1)

        def values(b, g, kb):
            pe = nc.tensor
            if kb == 0:
                if g == 0:
                    pe.wait_ge(gl, FM * b + 1)
                    pe.wait_ge(vf, TT * (b + 1))
                else:
                    pe.wait_ge(osd, NG * b + g)
            pe.wait_ge(ex, U * (NG * b + g) + 2 * kb + 2)
            for j in range(G):
                i = pe.matmul(Cb[32 * j:32 * j + 32, :], V[:, kb, g * G + j, :], Pr[:, (2 * kb + j // 2) % 4, j % 2, :],
                              start=(kb == 0), stop=(kb == TT - 1))
            i.then_inc(av, 1)

        def sums(b, g):
            pe = nc.tensor
            pe.wait_ge(osd, NG * b + g + 1)
            if g < 2:
                pe.wait_ge(mread, NG * b + 3 + g)
            else:
                pe.wait_ge(om, NG * b + g)
            for qb in range(TT):
                i = pe.matmul(Db[:, qb * G:(qb + 1) * G], oS[:, qb * P:(qb + 1) * P], selden[:, :],
                              start=True, stop=True)
            i.then_inc(den, 1)

        def spread(b, g):
            pe = nc.tensor
            pe.wait_ge(rc, NG * b + g + 1)
            for qb in range(TT):
                i = pe.transpose(Db[:, qb * P:(qb + 1) * P],
                                 recx[:, qb * P:(qb + 1) * P], ident[:, :])
            i.then_inc(rct, 1)

        def project(b, t):
            pe = nc.tensor
            if t == 0:
                pe.wait_ge(onh, NG * (b + 1))
                pe.wait_ge(onl, NG * (b + 1))
                pe.wait_ge(v_wst, 8)
                pe.wait_ge(g_w, 5)
                pe.wait_ge(ex, U * NG * (b + 1))
            ts = slice(t * P, (t + 1) * P)
            three(BB[t // 2][:, t % 2, 0:C],
                  [(oH[:, g, ts], oL[:, g, ts], WpH[:, g, :], WpL[:, g, :]) for g in range(NG)], C).then_inc(pj, 1)

        def step_all(b, more):
            pe = nc.tensor
            for g in range(NG):
                for u in range(U):
                    scores(b, g, u)
                    if g < 2:
                        row_max(b, g + 2, 2 * u)
                        row_max(b, g + 2, 2 * u + 1)
                    elif more:
                        if g == 2 and u == 2:
                            pe.wait_ge(xn1, TT * (b + 2))
                            pe.wait_ge(mxd, N1 * NG * (b + 1))
                        if g == 2 and 2 <= u < 5:
                            t_chunk(u - 2, b + 1, t1, t1f)
                        if g == 2 and u == 7:
                            qk_tile(b + 1, 0)
                        if g == 3 and u % 2 == 1:
                            qk_tile(b + 1, u // 2 + 1)
                    if u == 0 and g in (1, 2):
                        if g == 1:
                            pe.wait_ge(mread, NG * b + 2)
                        else:
                            pe.wait_ge(om, NG * b + 1)
                        max_rows(b, g + 1)
                    if u == 2 and g == 0:
                        pe.wait_ge(mread, NG * b + 1)
                        max_rows(b, 1)
                    if u == 1 and g > 0:
                        values(b, g - 1, TT - 1)
                    if u == 3 and g > 0:
                        sums(b, g - 1)
                    if u == 5 and g > 0:
                        spread(b, g - 1)
                    if u in (3, 5, 7):
                        values(b, g, (u - 3) // 2)
            values(b, NG - 1, TT - 1)
            if more:
                v_front(b + 1, 0)
            sums(b, NG - 1)
            if more:
                for t in range(1, TT):
                    v_front(b + 1, t)
            spread(b, NG - 1)
            for t in range(TT):
                project(b, t)
            if more:
                for n in range(PRE):
                    row_max(b + 1, 0, n)
            pe.wait_ge(xn2, TT * (b + 1))
            if more:
                pe.wait_ge(mxd, N1 * NG * (b + 1) + PRE)
            else:
                pe.wait_ge(mxd, N1 * NG * (b + 1))
            for c in range(3):
                t_chunk_m(c, b)
            pe.wait_ge(h2h, 2 * b + 2)
            pe.wait_ge(h2l, 2 * b + 2)
            pe.wait_ge(h2r, 2 * b + 2)
            for m in range(FM + 2):
                if m < FM:
                    up(b, m)
                    if more:
                        for g, n in MLP_P1[m]:
                            if (g, n) == (0, PRE):
                                pe.wait_ge(t2f, 3 * b + 4)
                            row_max(b + 1, g, n)
                if m == FM and more:
                    pe.wait_ge(gl, FM * b + FM)
                    max_rows(b + 1, 0)
                if m >= 2:
                    down(b, m - 2)

        def t_chunk_m(c, b):
            pe = nc.tensor
            if c == 2:
                pe.wait_ge(t2f, 3 * b + 2)
            for t in range(TT):
                i = pe.transpose(A[c % 2][:, t * P:(t + 1) * P], xs[:, t, c * P:(c + 1) * P], ident[:, :])
            i.then_inc(t2, 1)

        def up(b, m):
            pe = nc.tensor
            if m == 0:
                pe.wait_ge(osd, NG * (b + 1))
            elif m == 1:
                pe.wait_ge(om, NG * (b + 1))
            else:
                pe.wait_ge(gl, FM * b + m)
            n = slice(m * P, (m + 1) * P)
            three(CD[m % 2][:, :],
                  [(W1H[:, k, n], W1L[:, k, n], hMH[:, k, :], hML[:, k, :]) for k in range(KC)],
                  L, (W1R[:, n], hMR[:, :])).then_inc(f1, 1)

        def down(b, m):
            pe = nc.tensor
            if m == 0:
                pe.wait_ge(pjt, TT * (b + 1))
            pe.wait_ge(gs, FM * b + m + 1)
            s = m % NG
            for t in range(TT):
                ts = slice(t * P, (t + 1) * P)
                for k, (a, c) in enumerate(((oH, W2H), (oH, W2L), (oL, W2H))):
                    i = pe.matmul(BB[t // 2][:, t % 2, 0:C], a[:, s, ts], c[:, m, :],
                                  start=(m == 0 and k == 0), stop=(m == FM - 1 and k == 2))
            i.then_inc(f2, 1)

        @block.tensor
        def _(pe):
            mm = pe.matmul
            pe.wait_ge(g_init, 5)
            pe.wait_ge(a_silu, 1)
            for k in range(3):
                i = pe.transpose(Cb[0:96, k * B:(k + 1) * B], cS[:, k * 96:(k + 1) * 96], ident[0:B, 0:B])
            i.then_inc(pe_c, 1)
            pe.wait_ge(d_bias, 16 * 11)
            pe.wait_ge(v_bias, 1)
            pe.transpose(Db[:, 0:22], rows, ident[0:22, 0:22])
            pe.transpose(Db[:, 22:26], rem4x, ident[0:4, 0:4]).then_inc(pe_bias, 1)
            pe.wait_ge(v_c, 1)
            pe.wait_ge(d_wac, 16 * 6)
            for v in range(4):
                for c in range(3):
                    o = (v * 3 + c) * B
                    for k in range(3):
                        if c < KC:
                            i = mm(BB[0][:, 0, o:o + B], WaC[:, k, v, c * P:(c + 1) * P], cT[:, k, :],
                                   start=(k == 0), stop=(k == 2))
                        else:
                            for q in range(4):
                                i = mm(BB[0][q * REM:(q + 1) * REM, 0, o:o + B], WaC[:, k, v, KC * P:C], cT[:, k, :],
                                       start=(k == 0), stop=(k == 2))
            i.then_inc(pe_ada, 1)
            t_front(0)
            qk_front(0)
            pe.wait_ge(d_wag, 16 * 6)
            for v in range(2):
                for k in range(3):
                    i = mm(BB[1][0:B, v, 0:C], cT[:, k, :], WaG[:, k, v, :], start=(k == 0), stop=(k == 2))
            i.then_inc(pe_gate, 1)
            v_front(0, 0)
            v_front(0, 1)
            v_front(0, 2)
            v_front(0, 3)
            for n in range(N1):
                row_max(0, 0, n)
            max_rows(0, 0)
            for n in range(N1):
                row_max(0, 1, n)
            with pe.Fori(0, B - 1) as b:
                step_all(b, True)
            step_all(B - 1, False)

        def modulated(b, v, c, src, done):
            nc.scalar.activation(FT[:, c, :], src, ACT.Identity, bias=ada[:, v * 3 + c, bass.ds(b, 1)],
                                 scale=ada[:, (v + 1) * 3 + c, bass.ds(b, 1)]).then_inc(done, 1)

        def front_h(b):
            act = nc.scalar
            act.wait_ge(v_ada, 10)
            for c in range(3):
                front_hc(b, c)

        def front_hc(b, c):
            nc.scalar.wait_ge(t1, 3 * b + c + 1)
            modulated(b, 0, c, A[c % 2][:, :], t1f)

        def front_qk(b, m):
            act = nc.scalar
            n = qk_rows(m)
            act.wait_ge(qk, QKT * b + m + 1)
            if m >= 2:
                act.wait_ge(q3, QKT * b + m - 1)
                s = 3 if m % 2 == 0 else 2
                act.wait_ge(d_scr[m % 2], 16 * (s * b + m // 2))
            elif not (isinstance(b, int) and b == 0):
                act.wait_ge(d_scr[m % 2], 16 * (3 if m == 0 else 2) * b)
            bias = biasC[0:n, FM + m:FM + m + 1]
            act.activation(FQ[0:n, m % 2, :], A[(m + 1) % 2][0:n, :], ACT.Identity, bias=bias).then_inc(qkf, 1)
            act.activation(qk3[0:n, m % 2, 0, :], A[(m + 1) % 2][0:n, :], ACT.Identity, bias=bias).then_inc(qkf, 1)

        def exps(b, g, u):
            act = nc.scalar
            act.wait_ge(p2, U * (NG * b + g) + u + 1)
            if u >= 4:
                act.wait_ge(av, TT * (NG * b + g) + u // 2 - 1)
            elif g > 0:
                act.wait_ge(av, TT * (NG * b + g) + u // 2 - 1)
            act.activation(Pr[:, u % 4, :, :], BB[u % 2][:, :, :], ACT.Exp, scale=SCALE).then_inc(ex, 1)

        def take(b, g):
            act = nc.scalar
            act.wait_ge(av, TT * (NG * b + g + 1))
            if g > 0:
                act.wait_ge(onh, NG * b + g)
                act.wait_ge(onl, NG * b + g)
            act.activation(oS[:, :], Cb[:, :], ACT.Copy).then_inc(osd, 1)

        def act_body(b, more):
            act = nc.scalar
            for g in range(NG):
                for u in range(U):
                    exps(b, g, u)
                    if u == 2 and g > 0:
                        take(b, g - 1)
                    if more:
                        if g == 2 and 2 < u < 6:
                            front_hc(b + 1, u - 3)
                        if g == 3 and u % 2 == 0:
                            front_qk(b + 1, u // 2)
            if more:
                front_qk(b + 1, QKT - 1)
            take(b, NG - 1)
            if more:
                act.wait_ge(q3, QKT * (b + 2))
            for c in range(3):
                act.wait_ge(t2, 3 * b + c + 1)
                modulated(b, 2, c, A[c % 2][:, :], t2f)
            for m in range(FM):
                act.wait_ge(f1, FM * b + m + 1)
                if m >= 2:
                    act.wait_ge(gs, FM * b + m - 1)
                act.activation(FQ[:, m % 2, :], CD[m % 2][:, :], ACT.Gelu_apprx_tanh,
                               bias=biasC[:, m:m + 1]).then_inc(gl, 1)

        @block.scalar
        def _(act):
            act.wait_ge(d_c, 16)
            act.activation(cS, cS, ACT.Silu).then_inc(a_silu, 1)
            act.wait_ge(g_init, 10)
            act.activation(seed[:, 1:2], seed[:, 0:1], ACT.Copy).then_inc(gl, 1)
            act.activation(seed[:, 2:3], seed[:, 0:1], ACT.Copy).then_inc(t2f, 1)
            front_h(0)
            for m in range(QKT):
                front_qk(0, m)
            act.wait_ge(v_wst, 4)
            act.wait_ge(g_w, 1)
            with act.Fori(0, B - 1) as b:
                act_body(b, True)
            act_body(B - 1, False)

        def stats(b, t, src, done):
            nc.vector.bn_stats(st[:, t, :], src[:, t, 0:C]).then_inc(done, 1)

        def aggregate(b, done, step, agg):
            dve = nc.vector
            dve.wait_ge(done, TT * (b + 1))
            even, odd = 1, 4
            dve.tensor_tensor(mv[:, 0, :], st[:, :, even], st[:, :, odd], ALU.add).then_inc(step, 1)
            dve.tensor_tensor(mv[:, 1, :], st[:, :, even], st[:, :, odd], ALU.subtract).then_inc(step, 1)
            dve.tensor_tensor(mv[:, 2, :], st[:, :, even + 1], st[:, :, odd + 1], ALU.add).then_inc(step, 1)
            dve.wait_ge(step, 5 * b + 3)
            dve.tensor_scalar(mean[:, :], mv[:, 0, :], 0.5, None, ALU.mult).then_inc(step, 1)
            dve.scalar_tensor_tensor(out=mv[:, 3, :], in0=mv[:, 1, :], scalar=0.25, in1=mv[:, 1, :],
                                     op0=ALU.mult, op1=ALU.mult).then_inc(step, 1)
            dve.wait_ge(step, 5 * b + 5)
            dve.scalar_tensor_tensor(out=var[:, :], in0=mv[:, 2, :], scalar=1.0 / C, in1=mv[:, 3, :],
                                     op0=ALU.mult, op1=ALU.add).then_inc(agg, 1)

        def normed(b, w, src, ready, done):
            nc.vector.wait_ge(ready, b + 1)
            for t in range(TT):
                nc.vector.tensor_scalar(xs[:, t, C:3 * P].rearrange("p (a c) -> p a c", c=REM),
                                        src[:, t, KC * P:C].unsqueeze(1).to_broadcast([P, 3, REM]),
                                        mean[:, t:t + 1], rs[:, w, t:t + 1], ALU.subtract, ALU.mult).then_inc(xnr[w], 1)
            nc.vector.wait_ge(xnr[w], TT * (b + 1))
            for t in range(TT):
                nc.vector.tensor_scalar(xs[:, t, 0:C], src[:, t, 0:C], mean[:, t:t + 1], rs[:, w, t:t + 1],
                                        ALU.subtract, ALU.mult).then_inc(done, 1)

        def split_h(b, w, c):
            dve = nc.vector
            if w == 0:
                if c == 0 and not (isinstance(b, int) and b == 0):
                    dve.wait_ge(vv, TT * b)
                dve.wait_ge(t1f, 3 * b + c + 1)
            else:
                dve.wait_ge(t2f, 3 * b + c + 2)
            hh, hr, high, rest = (h1h, h1r, hAH, hAR) if w == 0 else (h2h, h2r, hMH, hMR)
            if c < KC:
                dve.tensor_copy(high[:, c, :], FT[:, c, :]).then_inc(hh, 1)
            else:
                dve.tensor_copy(rnd[:, :], FT[:, c, :]).then_inc(hr, 1)
                dve.wait_ge(hr, 2 * b + 1)
                dve.scalar_tensor_tensor(out=rest[:, :], in0=rnd[:, :].bitcast(f32), scalar=mask[:, 1:2],
                                         in1=FT[:, c, :], op0=ALU.mult, op1=ALU.add).then_inc(hr, 1)

        def second(b, m):
            n = qk_rows(m)
            nc.vector.wait_ge(qr, QKT * b + m + 1)
            nc.vector.tensor_copy(qk3[0:n, m % 2, 1, :], FT[0:n, m % 2, :]).then_inc(q2, 1)

        def take_v(b, t):
            dve = nc.vector
            dve.wait_ge(vv, TT * b + t + 1)
            if t == 0:
                if isinstance(b, int) and b == 0:
                    dve.wait_ge(v_wq, 5)
                else:
                    dve.wait_ge(av, TT * NG * b)
            dve.tensor_tensor(V[:, t, :, 0:D], A[t % 2][:, 0:C].rearrange("p (h d) -> p h d", h=H),
                              biasB[:, 2, :].rearrange("p (h d) -> p h d", h=H), ALU.add).then_inc(vf, 1)

        def maximum(b, g, n):
            dve = nc.vector
            dve.wait_ge(p1, N1 * (NG * b + g) + n + 1)
            if n == 0 and not (isinstance(b, int) and b == 0 and g < 2):
                dve.wait_ge(mt, NG * b + g - 1)
            dve.tensor_reduce(mx[:, g % 2, n:n + 1], A[n % 2][:, :], AX, ALU.max, negate=True).then_inc(mxd, 1)

        def max_parts(b, g):
            dve, i, s = nc.vector, NG * b + g, g % 2
            dve.wait_ge(mt, i + 1)
            if not (isinstance(b, int) and b == 0 and g < 2):
                dve.wait_ge(d_mrow[s], 48 * (2 * b + g // 2))
            dve.tensor_copy(mr[:, s, 0, :], Db[0:N1, 0:P]).then_inc(mstep, 1)
            dve.wait_ge(mstep, 3 * i + 1)
            dve.tensor_tensor(mres[:, :], Db[0:N1, 0:P], mr[:, s, 0, :], ALU.subtract).then_inc(mread, 1)
            dve.wait_ge(mread, i + 1)
            dve.tensor_copy(mr[:, s, 1, :], mres[:, :]).then_inc(mstep, 1)
            dve.wait_ge(mstep, 3 * i + 2)
            dve.tensor_tensor(mr[:, s, 2, :], mres[:, :], mr[:, s, 1, :], ALU.subtract).then_inc(mstep, 1)

        def invert(b, g):
            nc.vector.wait_ge(den, NG * b + g + 1)
            nc.vector.reciprocal(rec[:, :], Db[:, 0:N1]).then_inc(rinv, 1)
            nc.vector.wait_ge(rinv, NG * b + g + 1)
            nc.vector.tensor_copy(recx.rearrange("p (a c) -> p a c", c=32),
                                  rec[:, :].unsqueeze(2).to_broadcast([P, N1, 32])).then_inc(rc, 1)

        def normalize(b, g):
            dve, i = nc.vector, NG * b + g + 1
            dve.wait_ge(rct, i)
            dve.tensor_tensor(oS[:, :], oS[:, :], Db[:, :], ALU.mult).then_inc(om, 1)
            dve.wait_ge(om, i)
            dve.tensor_copy(oH[:, g, :], oS[:, :]).then_inc(onh, 1)

        def dve_body(b, more):
            dve = nc.vector
            for g in range(NG):
                for u in range(U):
                    if g < 2:
                        maximum(b, g + 2, 2 * u)
                        maximum(b, g + 2, 2 * u + 1)
                    if g == 0 and u == 2:
                        max_parts(b, 1)
                    if g in (1, 2) and u == 0:
                        max_parts(b, g + 1)
                    if more and g == 2 and u == 0:
                        normed(b + 1, 0, xs, g_rs1, xn1)
                    if more and g == 3 and u in (2, 4, 6):
                        second(b + 1, u // 2 - 1)
                    if g > 0 and u == 3:
                        invert(b, g - 1)
                    if g > 0 and u == 5:
                        normalize(b, g - 1)
                if more and g == 1:
                    dve.wait_ge(d_x, 16 * (b + 2))
                    for t in range(TT):
                        stats(b + 1, t, xs, ln1s)
                    aggregate(b + 1, ln1s, ln1a, ln1v)
                if more and g == 2:
                    for c in range(3):
                        split_h(b + 1, 0, c)
            if more:
                second(b + 1, 3)
                take_v(b + 1, 0)
                second(b + 1, 4)
            invert(b, NG - 1)
            if more:
                for t in range(1, TT):
                    take_v(b + 1, t)
            normalize(b, NG - 1)
            dve.wait_ge(d_gate, 16 * (b + 1))
            dve.wait_ge(g_x1, b + 1)
            for t in range(TT):
                dve.wait_ge(pj, TT * b + t + 1)
                dve.tensor_tensor(tmp[:, t % 2, :], BB[t // 2][:, t % 2, 0:C], gate[:, 0, :], ALU.mult).then_inc(pjt, 1)
                dve.wait_ge(pjt, TT * b + t + 1)
                dve.tensor_tensor(x1[:, t, :], x1[:, t, :], tmp[:, t % 2, :], ALU.add).then_inc(pjx, 1)
                dve.wait_ge(pjx, TT * b + t + 1)
                stats(b, t, x1, ln2s)
            aggregate(b, ln2s, ln2a, ln2v)
            if more:
                maximum(b + 1, 0, 0)
                maximum(b + 1, 0, 1)
                dve.wait_ge(t1, 3 * b + 6)
            normed(b, 1, x1, g_rs2, xn2)
            if more:
                for n in range(2, PRE):
                    maximum(b + 1, 0, n)
            for c in range(3):
                split_h(b, 1, c)
            for m in range(FM):
                if more:
                    for g, n in MLP_P1[m]:
                        maximum(b + 1, g, n)
                dve.wait_ge(gl, FM * b + m + 2)
                if m < NG:
                    dve.wait_ge(pj, TT * (b + 1))
                else:
                    dve.wait_ge(f2, FM * b + m - NG + 1)
                dve.tensor_copy(oH[:, m % NG, :], FQ[:, m % 2, :]).then_inc(gh, 1)
                dve.wait_ge(gh, FM * b + m + 1)
                dve.tensor_tensor(oL[:, m % NG, :], FQ[:, m % 2, :], oH[:, m % NG, :].bitcast(f32),
                                  ALU.subtract).then_inc(gs, 1)
            if more:
                max_parts(b + 1, 0)
            dve.wait_ge(f2, FM * (b + 1))
            dve.wait_ge(g_x2, b + 1)
            for t in range(TT):
                dve.tensor_tensor(tmp[:, t % 2, :], BB[t // 2][:, t % 2, 0:C], gate[:, 1, :], ALU.mult).then_inc(yt, 1)
                dve.wait_ge(yt, TT * b + t + 1)
                dve.tensor_tensor(x1[:, t, :], x1[:, t, :], tmp[:, t % 2, :], ALU.add).then_inc(yd, 1)

        @block.vector
        def _(dve):
            tc, tt, tsc, stt = dve.tensor_copy, dve.tensor_tensor, dve.tensor_scalar, dve.scalar_tensor_tensor
            dve.memset(FQ[:, :, :], 0.0).then_inc(v_init, 1)
            dve.memset(KS[96:P, :, :], 1.0).then_inc(v_init, 1)
            dve.memset(oS[:, :], 0.0).then_inc(yd, 1)
            dve.wait_ge(d_x, 16)
            for t in range(TT):
                stats(0, t, xs, ln1s)
            aggregate(0, ln1s, ln1a, ln1v)
            dve.wait_ge(pe_c, 1)
            tc(cT[:, :, :], Cb[0:96, 0:3 * B].rearrange("p (k b) -> p k b", k=3)).then_inc(v_c, 1)
            dve.wait_ge(d_bias, 16 * 11)
            tc(rem4x.rearrange("p (a c) -> p a c", a=4), rem4.unsqueeze(1).to_broadcast([4, 4, REM])).then_inc(v_bias, 1)
            normed(0, 0, xs, g_rs1, xn1)
            dve.wait_ge(pe_bias, 1)
            tc(biasC[:, :], Db[:, 0:26]).then_inc(v_bias, 1)
            dve.wait_ge(d_wq, 16 * KC)
            tc(WqH[:, :, :], WqS).then_inc(v_wq, 1)
            dve.wait_ge(v_wq, 1)
            tt(WqL[:, :, :], WqS, WqH[:, :, :].bitcast(f32), ALU.subtract).then_inc(v_wq, 1)
            dve.wait_ge(d_wqr, 16 * 4)
            tc(WqR[:, :], X1S[:, 0:3 * C]).then_inc(v_wq, 1)
            dve.wait_ge(v_wq, 3)
            dve.wait_ge(g_init, 8)
            stt(out=WqR[:, :], in0=WqR[:, :].bitcast(f32), scalar=mask[:, 0:1], in1=X1S[:, 0:3 * C],
                op0=ALU.mult, op1=ALU.add).then_inc(v_wq, 1)
            dve.wait_ge(v_bias, 2)
            dve.wait_ge(pe_ada, 1)
            for v in range(4):
                tt(ada[:, 3 * v:3 * v + 2, :], BB[0][:, 0, 3 * v * B:(3 * v + 2) * B].rearrange("p (c b) -> p c b", c=2),
                   biasC[:, FM + QKT + 2 * v:FM + QKT + 2 * v + 2].unsqueeze(2).to_broadcast([P, 2, B]),
                   ALU.add).then_inc(v_ada, 1)
                tt(ada[:, 3 * v + 2, :], BB[0][:, 0, (3 * v + 2) * B:(3 * v + 3) * B],
                   biasC[:, 22 + v:23 + v].to_broadcast([P, B]), ALU.add).then_inc(v_ada, 1)
            dve.wait_ge(v_ada, 8)
            for v in (1, 3):
                tsc(ada[:, 3 * v:3 * v + 3, :], ada[:, 3 * v:3 * v + 3, :], 1.0, None, ALU.add).then_inc(v_ada, 1)
            for c in range(3):
                split_h(0, 0, c)
            dve.memset(V[:, :, :, D:32], 0.0).then_inc(v_wq, 1)
            dve.wait_ge(v_wq, 5)
            dve.memset(V[:, :, :, D:D + 1], 1.0).then_inc(v_wst, 1)
            for m in range(QKT):
                second(0, m)
            dve.wait_ge(pe_gate, 1)
            dve.wait_ge(d_bgate, 16 * 2)
            tt(gateS, BB[1][0:B, :, 0:C], tmp[0:B, :, :], ALU.add).then_inc(v_gate, 1)
            dve.wait_ge(d_bb, 16 * 3)
            for t in range(TT):
                take_v(0, t)
            for n in range(N1):
                maximum(0, 0, n)
            max_parts(0, 0)
            dve.wait_ge(d_w1, 16 * 6)
            tc(W1H[:, :, :], W1S[:, 0:KC, :]).then_inc(v_wst, 1)
            tc(W1R[:, :], W1S[:, KC, :]).then_inc(v_wst, 1)
            dve.wait_ge(v_wst, 3)
            stt(out=W1R[:, :], in0=W1R[:, :].bitcast(f32), scalar=mask[:, 0:1], in1=W1S[:, KC, :],
                op0=ALU.mult, op1=ALU.add).then_inc(v_wst, 1)
            for r, (high, low, k) in enumerate(STAGED):
                dve.wait_ge(d_stage, STAGED_AT[r])
                tc(high, x1[:, 0:k, :]).then_inc(v_wst, 1)
                for n in range(4 * r, 4 * r + 4):
                    maximum(0, 1, n)
            with dve.Fori(0, B - 1) as b:
                dve_body(b, True)
            dve_body(B - 1, False)

        def inverse_std(b, w, ready, done):
            gp = nc.gpsimd
            gp.wait_ge(ready, b + 1)
            if isinstance(b, int) and b == 0 and w == 0:
                gp.wait_ge(g_init, 11)
            gp.tensor_tensor(ve[:, :], var[:, :], epsT[:, :], ALU.add).then_inc(g_ve[w], 1)
            gp.wait_ge(g_ve[w], b + 1)
            gp.tensor_tensor(rs[:, w, :], ve[:, :], half[:, :], ALU.pow).then_inc(done, 1)

        def low_h(b, w):
            gp = nc.gpsimd
            hh, hl, high, low = (h1h, h1l, hAH, hAL) if w == 0 else (h2h, h2l, hMH, hML)
            for c in range(KC):
                gp.wait_ge(hh, KC * b + c + 1)
                gp.tensor_tensor(low[:, c, :], FT[:, c, :], high[:, c, :].bitcast(f32), ALU.subtract).then_inc(hl, 1)

        def residual(b, m):
            n = qk_rows(m)
            nc.gpsimd.wait_ge(qkf, 2 * (QKT * b + m + 1))
            nc.gpsimd.tensor_tensor(FT[0:n, m % 2, :], FQ[0:n, m % 2, :], qk3[0:n, m % 2, 0, :], ALU.subtract).then_inc(qr, 1)

        def third(b, m):
            n = qk_rows(m)
            nc.gpsimd.wait_ge(q2, QKT * b + m + 1)
            nc.gpsimd.tensor_tensor(qk3[0:n, m % 2, 2, :], FT[0:n, m % 2, :], qk3[0:n, m % 2, 1, :], ALU.subtract).then_inc(q3, 1)

        def low_o(b, g):
            nc.gpsimd.wait_ge(onh, NG * b + g + 1)
            nc.gpsimd.tensor_tensor(oL[:, g, :], oS[:, :], oH[:, g, :].bitcast(f32), ALU.subtract).then_inc(onl, 1)

        def gp_body(b, more):
            gp = nc.gpsimd
            gp.wait_ge(d_gate, 16 * (b + 1))
            if isinstance(b, int) is False or b == 0:
                gp.wait_ge(d_bb, 16 * 3)
            gp.tensor_tensor(gb[:, :, :], gate[:, :, :], biasB[:, 0:2, :], ALU.mult).then_inc(g_gb, 1)
            gp.wait_ge(g_gb, b + 1)
            gp.wait_ge(d_x1, 16 * (b + 1))
            gp.tensor_tensor(x1[:, :, :], x1[:, :, :], gb[:, 0, :].unsqueeze(1).to_broadcast([P, TT, C]), ALU.add).then_inc(g_x1, 1)
            low_o(b, 0)
            if more:
                inverse_std(b + 1, 0, ln1v, g_rs1)
            low_o(b, 1)
            if more:
                low_h(b + 1, 0)
                residual(b + 1, 0)
                residual(b + 1, 1)
                third(b + 1, 0)
            low_o(b, 2)
            if more:
                residual(b + 1, 2)
                third(b + 1, 1)
                residual(b + 1, 3)
                third(b + 1, 2)
                residual(b + 1, 4)
                third(b + 1, 3)
                third(b + 1, 4)
            low_o(b, 3)
            inverse_std(b, 1, ln2v, g_rs2)
            low_h(b, 1)
            gp.wait_ge(xn2, TT * (b + 1))
            gp.tensor_tensor(x1[:, :, :], x1[:, :, :], gb[:, 1, :].unsqueeze(1).to_broadcast([P, TT, C]), ALU.add).then_inc(g_x2, 1)

        @block.gpsimd
        def _(gp):
            gp.memset(ident[:, :], 0.0).then_inc(g_init, 1)
            gp.memset(selden[:, :], 0.0).then_inc(g_init, 1)
            gp.memset(mask[:, :], 0.0).then_inc(g_init, 1)
            gp.wait_ge(g_init, 3)
            gp.affine_select(out=ident[:, :], in_=ident[:, :], compare_op=ALU.not_equal, fill=1.0,
                             base=0, pattern=[[-1, P]], channel_multiplier=1).then_inc(g_init, 1)
            gp.affine_select(out=selden[:, :], in_=selden[:, :], compare_op=ALU.not_equal, fill=1.0,
                             base=-D, pattern=[[-32, G]], channel_multiplier=1).then_inc(g_init, 1)
            for n, (q, col) in enumerate(((slice(64, P), 0), (slice(32, 64), 1), (slice(96, P), 1))):
                gp.wait_ge(g_init, 5 + n)
                gp.memset(mask[q, col:col + 1], -1.0).then_inc(g_init, 1)
            gp.wait_ge(g_init, 8)
            gp.memset(half[:, :], -0.5).then_inc(g_init, 1)
            gp.memset(seed[:, :], 0.0).then_inc(g_init, 1)
            gp.memset(epsT[:, :], EPS).then_inc(g_init, 1)
            inverse_std(0, 0, ln1v, g_rs1)
            low_h(0, 0)
            residual(0, 0)
            residual(0, 1)
            for m in range(QKT):
                third(0, m)
                if m + 2 < QKT:
                    residual(0, m + 2)
            gp.wait_ge(v_wst, 4)
            gp.tensor_tensor(W1L[:, :, :], W1S[:, 0:KC, :], W1H[:, :, :].bitcast(f32), ALU.subtract).then_inc(g_w, 1)
            gp.wait_ge(d_gs, 16)
            gp.memset(x1[:, :, :], 0.0).then_inc(g_x0, 1)
            gp.wait_ge(g_x0, 1)
            wp = w_proj.rearrange("(g j d) n -> j d g n", g=NG, j=G)
            for j in range(G):
                gp.dma_start(x1[32 * j:32 * j + D, :, :], wp[j]).then_inc(d_stage, 16)
            w2 = w_fc2.rearrange("(k p) n -> p k n", p=P)
            for r, (high, low, k) in enumerate(STAGED):
                gp.wait_ge(v_wst, 5 + r)
                gp.tensor_tensor(low, x1[:, 0:k, :], high.bitcast(f32), ALU.subtract).then_inc(g_w, 1)
                if r < 3:
                    gp.wait_ge(g_w, 2 + r)
                    k1 = STAGED[r + 1][2]
                    gp.dma_start(x1[:, 0:k1, :], w2[:, 4 * r:4 * r + k1, :]).then_inc(d_stage, 16)
            with gp.Fori(0, B - 1) as b:
                gp_body(b, True)
            gp_body(B - 1, False)


_INS = {"x": "x", "cond": "cond_1152", "w_qkv": "L0_cond_W_qkv", "b_qkv": "L0_cond_b_qkv", "w_proj": "L0_cond_W_proj",
        "b_proj": "L0_cond_b_proj", "w_fc1": "L0_cond_W_fc1", "b_fc1": "L0_cond_b_fc1", "w_fc2": "L0_cond_W_fc2",
        "b_fc2": "L0_cond_b_fc2", "w_ada": "L0_cond_W_ada", "b_ada": "L0_cond_b_ada"}


def kernel(**inputs):
    import numpy as _np
    import concourse.bacc as _bacc
    from concourse import mybir as _mybir
    from concourse.bass_utils import run_bass_kernel_spmd as _run

    nc = _bacc.Bacc("TRN2", target_bir_lowering=False, num_devices=1)
    arrays, args = {}, {}
    for arg, name in _INS.items():
        a = _np.ascontiguousarray(inputs[name])
        arrays[f"in_{arg}"] = a
        args[arg] = nc.dram_tensor(f"in_{arg}", a.shape, _mybir.dt.from_np(a.dtype), kind="ExternalInput").ap()
    o = nc.dram_tensor("out_0", (B, L, C), _mybir.dt.float32, kind="ExternalOutput").ap()
    build(nc, out=o, **args)
    r = _run(nc, [arrays], core_ids=[0])
    return r.results[0]["out_0"]
```

```python
import concourse.bass as bass
from concourse import mybir
from contextlib import ExitStack

B, L, C = 4, 512, 288
H = 16
D = C // H
FF = 4 * C
EPS = 1e-6
SCALE = float(D) ** -0.5
P = 128
TT = L // P
KC = C // P
REM = C - KC * P
assert 4 * REM == P
G = 4
NG = H // G
SLOTS = P // D
QKT = -(-2 * H // SLOTS)
ORDER = (0, 2, 1, 3, 4)
QB = 3
PER = [len(range(i, QKT, QB)) for i in range(QB)]
QROWS = 6 * D
MROW = QROWS
FM = FF // P
BC = FM + QKT + 6 * 3
U = 2 * TT
N1 = G * TT


def qk_rows(m):
    return min(SLOTS, 2 * H - m * SLOTS) * D


def build(nc, x, cond, w_qkv, b_qkv, w_proj, b_proj, w_fc1, b_fc1, w_fc2, b_fc2, w_ada, b_ada, out):
    f32, f32r, bf16 = mybir.dt.float32, mybir.dt.float32r, mybir.dt.bfloat16
    ALU = mybir.AluOpType
    ACT = mybir.ActivationFunctionType
    AX = mybir.AxisListType.X

    ctx = ExitStack()
    with ctx:
        def sb(name, shape, dt):
            return ctx.enter_context(nc.sbuf_tensor(name, shape, dt))

        def sem(name):
            return ctx.enter_context(nc.semaphore(name))

        WqH, WqL, WqR = sb("WqH", [P, KC, 3 * C], f32r), sb("WqL", [P, KC, 3 * C], f32r), sb("WqR", [P, 3 * C], f32r)
        W1H, W1L, W1R = sb("W1H", [P, KC, FF], f32r), sb("W1L", [P, KC, FF], f32r), sb("W1R", [P, FF], f32r)
        W2H, W2L = sb("W2H", [P, FM, C], f32r), sb("W2L", [P, FM, C], f32r)
        WpH, WpL = sb("WpH", [P, NG, C], f32r), sb("WpL", [P, NG, C], f32r)
        QS, KS = sb("QS", [P, H, L], bf16), sb("KS", [P, H, L], bf16)
        Pr = sb("Pr", [P, 4, 2, L], f32)
        V = sb("V", [P, TT, H, 32], f32)
        qk3 = sb("qk3", [P, QB, 3, L], bf16)
        FT = sb("FT", [P, 3, L], f32)
        FQ = sb("FQ", [P, 2, L], f32)
        rnd = sb("rnd", [P, L], f32r)
        hAH, hAL, hAR = sb("hAH", [P, KC, L], f32r), sb("hAL", [P, KC, L], f32r), sb("hAR", [P, L], f32r)
        hMH, hML, hMR = sb("hMH", [P, KC, L], f32r), sb("hML", [P, KC, L], f32r), sb("hMR", [P, L], f32r)
        oH, oL = sb("oH", [P, NG, L], f32r), sb("oL", [P, NG, L], f32r)
        oS = sb("oS", [P, L], f32)
        xs = sb("xs", [P, TT, 3 * P], f32)
        x1 = sb("x1", [P, TT, C], f32)
        tmp = sb("tmp", [P, 2, C], f32)
        gate = sb("gate", [P, 2, C], f32)
        gb = sb("gb", [P, 2, C], f32)
        biasB = sb("biasB", [P, 3, C], f32)
        ident = sb("ident", [P, P], f32)
        selden = sb("selden", [P, G], f32)
        mask = sb("mask", [P, 2], f32)
        biasC = sb("biasC", [P, BC], f32)
        ada = sb("ada", [P, 12, B], f32)
        cT = sb("cT", [96, 3, B], f32)
        st, mv, rs, half = sb("st", [P, TT, 6], f32), sb("mv", [P, 4, TT], f32), sb("rs", [P, 2, TT], f32), sb("half", [P, TT], f32)
        mean, var = sb("mean", [P, TT], f32), sb("var", [P, TT], f32)
        epsT, ve, seed = sb("epsT", [P, TT], f32), sb("ve", [P, TT], f32), sb("seed", [P, 4], f32)
        mx = sb("mx", [P, 2, N1], f32)
        rec = sb("rec", [P, N1], f32)
        mr = sb("mr", [16, 2, 3, P], bf16)
        mres = sb("mres", [16, P], f32)
        QSF = QS[:, :, :].rearrange("p a b -> p (a b)").bitcast(f32)
        KSF = KS[:, :, :].rearrange("p a b -> p (a b)").bitcast(f32)
        cS, cA = FT[0:B, 0, 0:C], FT[0:B, 1, 0:C]
        rows, adaR, adaX = FQ[0:FM + QKT, 0, 0:P], FQ[0:6, 1, 0:C], FQ[0:6, 1, C:C + P]
        recx = tmp[:, :, :].rearrange("p a b -> p (a b)")[:, 0:L]
        gateS = x1[0:B, 0:2, :]
        PrF = Pr[:, :, :, :].rearrange("p a b c -> p (a b c)")
        WaC = PrF[0:96, 0:12 * C].rearrange("p (k v n) -> p k v n", k=3, v=4)
        WaG = KSF[0:96, 0:6 * C].rearrange("p (k v n) -> p k v n", k=3, v=2)
        WaR = KSF[0:96, 6 * C:6 * C + 12 * P].rearrange("p (k v n) -> p k v n", k=3, v=4)
        WpS = QSF[:, 0:NG * C].rearrange("p (k n) -> p k n", k=NG)
        W2S = QSF[:, NG * C:(NG + FM) * C].rearrange("p (k n) -> p k n", k=FM)
        W1S = PrF[:, 0:3 * FF].rearrange("p (k n) -> p k n", k=3)
        WqS = V[:, :, :, :].rearrange("p a b c -> p (a b c)")[:, 0:2 * 3 * C].rearrange("p (k n) -> p k n", k=2)
        X1S = x1[:, :, :].rearrange("p a b -> p (a b)")

        scr = nc.dram_tensor("qk_scratch", (3, 2 * H * D, L), bf16, kind="Internal").ap()
        gscr = nc.dram_tensor("gate_scratch", (B, 2, C), f32, kind="Internal").ap()

        A = [ctx.enter_context(nc.psum_tensor(f"A{i}", [P, L], f32)) for i in range(2)]
        BB = [ctx.enter_context(nc.psum_tensor(f"B{i}", [P, 2, L], f32)) for i in range(2)]
        Cb = ctx.enter_context(nc.psum_tensor("Cb", [P, L], f32))
        Db = ctx.enter_context(nc.psum_tensor("Db", [P, L], f32))
        CD = [Cb, Db]

        d_x, d_x1, d_gate = sem("d_x"), sem("d_x1"), sem("d_gate")
        d_c, d_bias, d_bb, d_bgate, d_wac, d_wag, d_wq, d_wqr, d_w1, d_wp, d_w2, d_gs = (sem(n) for n in (
            "d_c", "d_bias", "d_bb", "d_bgate", "d_wac", "d_wag", "d_wq", "d_wqr", "d_w1", "d_wp", "d_w2", "d_gs"))
        d_scr = [sem(f"d_scr{i}") for i in range(QB)]
        d_stk = [sem(f"d_stk{i}") for i in range(NG)]
        d_mrow = [sem(f"d_mrow{i}") for i in range(2)]
        d_out = sem("d_out")
        pe_c, pe_bias, pe_ada, pe_gate = sem("pe_c"), sem("pe_bias"), sem("pe_ada"), sem("pe_gate")
        t1, qk, vv, p1, mt, p2, av, den, rct, pj, t2, f1, f2 = (sem(n) for n in (
            "t1", "qk", "vv", "p1", "mt", "p2", "av", "den", "rct", "pj", "t2", "f1", "f2"))
        a_silu, t1f, t2f, qkf, ex, osd, gl = (sem(n) for n in ("a_silu", "t1f", "t2f", "qkf", "ex", "osd", "gl"))
        v_init, v_c, v_bias, v_ada, v_gate, v_wq, v_war, v_wp, v_w2, v_w1, g_one = (sem(n) for n in (
            "v_init", "v_c", "v_bias", "v_ada", "v_gate", "v_wq", "v_war", "v_wp", "v_w2", "v_w1", "g_one"))
        ln1s, ln1v, ln2s, ln2v, xn1, xn2 = (sem(n) for n in ("ln1s", "ln1v", "ln2s", "ln2v", "xn1", "xn2"))
        h1h, h1r, h2h, h2r, qr, q2, vf, mxd, mread, mstep, rc, om, onh, onl3, pjt, pjx, gs, yt, yd = (sem(n) for n in (
            "h1h", "h1r", "h2h", "h2r", "qr", "q2", "vf", "mxd", "mread", "mstep", "rc", "om", "onh", "onl3", "pjt", "pjx",
            "gs", "yt", "yd"))
        g_init, g_rs1, g_rs2, h1l, h2l, q3, onl, g_gb, g_x1, g_x2, g_wp, g_w1 = (sem(n) for n in (
            "g_init", "g_rs1", "g_rs2", "h1l", "h2l", "q3", "onl", "g_gb", "g_x1", "g_x2", "g_wp", "g_w1"))
        g_ve = [sem("g_ve1"), sem("g_ve2")]
        rinv, xnr, ln1a, ln2a = sem("rinv"), [sem("xnr1"), sem("xnr2")], sem("ln1a"), sem("ln2a")

        block = ctx.enter_context(nc.Block())

        PRE = 2
        REST = [(0, n) for n in range(PRE, N1)] + [(1, n) for n in range(N1)]
        MLP_P1 = [REST[len(REST) * m // FM:len(REST) * (m + 1) // FM] for m in range(FM)]
        ROWS_AT = 6
        assert (0, N1 - 1) in sum(MLP_P1[:ROWS_AT + 1], [])

        def load_gate(sp, b):
            sp.dma_start(gate[:, :, :], gscr[b].partition_broadcast(P)).then_inc(d_gate, 16)

        def load_x1(sp, b):
            sp.dma_start(x1[:, :, :], x[b].rearrange("(t p) c -> p t c", p=P)).then_inc(d_x1, 16)

        def mrow(sp, b, g):
            sp.wait_ge(mstep, 3 * (NG * b + g + 1))
            for j in range(3):
                sp.dma_start(QS[MROW + j:MROW + j + 1, g * G:(g + 1) * G, :], mr[:, g % 2, j, :]).then_inc(d_mrow[g % 2], 16)

        def parts_out(sp, b, i):
            m = ORDER[i]
            sp.wait_ge(q3, QKT * b + i + 1)
            r, n = m * SLOTS * D, qk_rows(m)
            sp.dma_start(scr[:, r:r + n, :].rearrange("j r t -> r j t"), qk3[0:n, i % QB, :, :]).then_inc(d_scr[i % QB], 16)

        def tiles_there(sp, count, n):
            for k in range(min(n, QB)):
                sp.wait_ge(d_scr[k], count[k, n])

        def front(sp, b):
            snap = (lambda v: v) if isinstance(b, int) else (lambda v: sp.snap(sp.to_reg(v)))
            count = {(k, n): snap(16 * (PER[k] * b + len(range(k, n, QB)))) for n in (2, 4, 5) for k in range(min(n, QB))}
            read = [None if isinstance(b, int) and b == 0 else snap(U * (NG * (b - 1) + g + 1)) for g in range(NG)]
            for i in range(3):
                parts_out(sp, b, i)
            if read[0] is not None:
                sp.wait_ge(p2, read[0])
            tiles_there(sp, count, 2)
            stacks(sp, 0, None, (0, 1, 2))
            parts_out(sp, b, 3)
            stacks(sp, 0, None, (3, 4, 5))
            parts_out(sp, b, 4)
            tiles_there(sp, count, 4)
            for g in range(1, NG):
                if g == NG - 1:
                    tiles_there(sp, count, 5)
                stacks(sp, g, read[g])

        def stacks(sp, g, read, some=range(6)):
            q0, k0 = g * G * D, (H + g * G) * D

            def part(j, r0):
                return scr[j, r0:r0 + G * D, :].rearrange("(h r) t -> r h t", r=D)

            hs = slice(g * G, (g + 1) * G)
            if read is not None:
                sp.wait_ge(p2, read)
            for i in some:
                j, k = ((0, 0), (0, 1), (0, 2), (1, 0), (1, 1), (2, 0))[i]
                sp.dma_start(QS[i * D:(i + 1) * D, hs, :], part(j, q0)).then_inc(d_stk[g], 16)
                sp.dma_start(KS[i * D:(i + 1) * D, hs, :], part(k, k0)).then_inc(d_stk[g], 16)

        def body(sp, b, more):
            mrow(sp, b, 1)
            if more:
                sp.wait_ge(yd, 2 * b + 1)
                sp.wait_ge(t1, 3 * b + 3)
                sp.wait_ge(v_init, 2)
                sp.dma_start(xs[:, :, 0:C], x[b + 1].rearrange("(t p) c -> p t c", p=P)).then_inc(d_x, 16)
            for g in (2, 3):
                mrow(sp, b, g)
            if more:
                front(sp, b + 1)
                mrow(sp, b + 1, 0)
            for i in range(2):
                sp.wait_ge(yd, 2 * b + i + 3)
                sp.wait_ge(v_init, 2)
                sp.dma_start(out[b, i * 2 * P:(i + 1) * 2 * P, :].rearrange("(t p) c -> p t c", p=P),
                             x1[:, 2 * i:2 * i + 2, :]).then_inc(d_out, 16)
            if more:
                load_gate(sp, b + 1)
                sp.wait_ge(d_out, 16 * 2 * (b + 1))
                sp.wait_ge(v_init, 2)
                load_x1(sp, b + 1)

        @block.sync
        def _(sp):
            sp.dma_start(cS, cond).then_inc(d_c, 16)
            sp.dma_start(xs[:, :, 0:C], x[0].rearrange("(t p) c -> p t c", p=P)).then_inc(d_x, 16)
            wa = w_ada.rearrange("(k p) (s n) -> p k s n", p=96, n=C)
            for k in range(3):
                sp.dma_start(WaC[:, k, 0:2, :], wa[:, k, 0:2, :]).then_inc(d_wac, 16)
                sp.dma_start(WaC[:, k, 2:4, :], wa[:, k, 3:5, :]).then_inc(d_wac, 16)
            sp.wait_ge(v_init, 1)
            sp.dma_start(FQ[0:6, 1, 0:C], b_ada.rearrange("(s n) -> s n", s=6)).then_inc(d_bias, 16)
            sp.dma_start(FQ[0:FM, 0, 0:P], b_fc1.rearrange("(m p) -> m p", p=P)).then_inc(d_bias, 16)
            n = (2 * C) // (SLOTS * D)
            sp.dma_start(FQ[FM:FM + n, 0, 0:SLOTS * D], b_qkv[0:n * SLOTS * D].rearrange("(m p) -> m p", m=n)).then_inc(d_bias, 16)
            sp.dma_start(FQ[FM + n:FM + n + 1, 0, 0:2 * C - n * SLOTS * D],
                         b_qkv[n * SLOTS * D:2 * C].rearrange("(o p) -> o p", o=1)).then_inc(d_bias, 16)
            wq = w_qkv[0:KC * P, :].rearrange("(k p) n -> p k n", p=P)
            for k in range(KC):
                sp.dma_start(WqS[:, k, :], wq[:, k, :]).then_inc(d_wq, 16)
            for q in range(4):
                sp.dma_start(X1S[q * REM:(q + 1) * REM, 0:3 * C], w_qkv[KC * P:C, :]).then_inc(d_wqr, 16)
            for v, s in enumerate((2, 5)):
                sp.dma_start(WaG[:, :, v, :], wa[:, :, s, :]).then_inc(d_wag, 16)
            sp.wait_ge(v_init, 2)
            wp = w_proj.rearrange("(g j d) n -> j d g n", g=NG, j=G)
            for j in range(G):
                sp.dma_start(WpS[32 * j:32 * j + D, :, :], wp[j]).then_inc(d_wp, 16)
            sp.dma_start(W2S, w_fc2.rearrange("(k p) n -> p k n", p=P)).then_inc(d_w2, 16)
            for i, s in enumerate((2, 5)):
                sp.dma_start(tmp[0:B, i, :], b_ada[s * C:(s + 1) * C].partition_broadcast(B)).then_inc(d_bgate, 16)
            for i, v in enumerate((b_proj[:], b_fc2[:], b_qkv[2 * C:3 * C])):
                sp.dma_start(biasB[:, i, :], v.partition_broadcast(P)).then_inc(d_bb, 16)
            sp.wait_ge(pe_ada, 1)
            w1 = w_fc1[0:KC * P, :].rearrange("(k p) n -> p k n", p=P)
            for k in range(KC):
                sp.dma_start(W1S[:, k, :], w1[:, k, :]).then_inc(d_w1, 16)
            for q in range(4):
                sp.dma_start(W1S[q * REM:(q + 1) * REM, KC, :], w_fc1[KC * P:C, :]).then_inc(d_w1, 16)
            sp.wait_ge(pe_gate, 1)
            sp.wait_ge(g_wp, 1)
            sp.wait_ge(v_w2, 4)
            sp.wait_ge(g_one, 1)
            front(sp, 0)
            sp.wait_ge(v_gate, 1)
            sp.dma_start(gscr[:, :, :], gateS).then_inc(d_gs, 16)
            sp.wait_ge(d_gs, 16)
            load_gate(sp, 0)
            mrow(sp, 0, 0)
            load_x1(sp, 0)
            with sp.Fori(0, B - 1) as b:
                body(sp, b, True)
            body(sp, B - 1, False)
            sp.wait_ge(d_out, 16 * 2 * B)

        def three(o, groups, N, tail=None):
            i, first = None, True
            for (lh, ll, rh, rl) in groups:
                for a, c in ((lh, rh), (lh, rl), (ll, rh)):
                    last = tail is None and a is ll and lh is groups[-1][0]
                    i = nc.tensor.matmul(o, a, c, start=first, stop=last)
                    first = False
            if tail is not None:
                i = nc.tensor.matmul(o, tail[0], tail[1], start=False, stop=True)
            return i

        def t_chunk(c, b, done, read):
            pe = nc.tensor
            if c == 2:
                pe.wait_ge(read, 3 * b + 1)
            for t in range(TT):
                i = pe.transpose(A[c % 2][:, t * P:(t + 1) * P], xs[:, t, c * P:(c + 1) * P], ident[:, :])
            i.then_inc(done, 1)

        def qk_tile(b, i):
            pe, m = nc.tensor, ORDER[i]
            if i == 0:
                pe.wait_ge(t1f, 3 * b + 2)
                pe.wait_ge(v_wq, 4)
                pe.wait_ge(h1h, 2 * b + 2)
                pe.wait_ge(h1l, 2 * b + 2)
                pe.wait_ge(h1r, 2 * b + 2)
            if i == 1:
                pe.wait_ge(t1f, 3 * b + 3)
            if i >= 2:
                pe.wait_ge(qr, QKT * b + i - 1)
            r, n = m * SLOTS * D, qk_rows(m)
            three(A[(i + 1) % 2][0:n, :],
                  [(WqH[:, k, r:r + n], WqL[:, k, r:r + n], hAH[:, k, :], hAL[:, k, :]) for k in range(KC)],
                  L, (WqR[:, r:r + n], hAR[:, :])).then_inc(qk, 1)

        def v_front(b, t):
            pe = nc.tensor
            if t < 2:
                pe.wait_ge(qr, QKT * b + QKT - 1 + t)
            else:
                pe.wait_ge(vf, TT * b + t - 1)
            ts, n = slice(t * P, (t + 1) * P), slice(2 * C, 3 * C)
            three(A[t % 2][:, 0:C],
                  [(hAH[:, k, ts], hAL[:, k, ts], WqH[:, k, n], WqL[:, k, n]) for k in range(KC)],
                  C, (hAR[:, ts], WqR[:, n])).then_inc(vv, 1)

        def row_max(b, g, n):
            pe = nc.tensor
            h, qb = g * G + n // TT, n % TT
            if n == 0:
                pe.wait_ge(d_stk[g], 192 * (b + 1))
            if n >= 2:
                pe.wait_ge(mxd, N1 * (NG * b + g) + n - 1)
            elif g == 0:
                pe.wait_ge(vf, TT * b + 3 + n)
            else:
                pe.wait_ge(mxd, N1 * (NG * b + g))
                if g == 2:
                    pe.wait_ge(t2f, 3 * b + 1)
            pe.matmul(A[n % 2][:, :], QS[0:QROWS, h, qb * P:(qb + 1) * P], KS[0:QROWS, h, :],
                      start=True, stop=True).then_inc(p1, 1)

        def max_rows(b, g):
            nc.tensor.wait_ge(mxd, N1 * (NG * b + g + 1))
            nc.tensor.transpose(Db[0:N1, 0:P], mx[:, g % 2, :], ident[:, :]).then_inc(mt, 1)

        def scores(b, g, u):
            pe = nc.tensor
            kb, hp = u // 2, u % 2
            if u == 0:
                pe.wait_ge(d_mrow[g % 2], 48 * (2 * b + g // 2 + 1))
            if g == 0 and u < 2:
                pe.wait_ge(yd, 2 * b + u + 1)
            else:
                pe.wait_ge(ex, U * (NG * b + g) + u - 1)
            for j in range(2):
                h = g * G + 2 * hp + j
                i = pe.matmul(BB[u % 2][:, j, :], KS[0:MROW + 3, h, kb * P:(kb + 1) * P], QS[0:MROW + 3, h, :],
                              start=True, stop=True)
            i.then_inc(p2, 1)

        def values(b, g, kb):
            pe = nc.tensor
            if kb == 0:
                if g == 0:
                    pe.wait_ge(gl, 2 * FM * b + 1)
                    pe.wait_ge(vf, TT * (b + 1))
                else:
                    pe.wait_ge(osd, NG * b + g)
            pe.wait_ge(ex, U * (NG * b + g) + 2 * kb + 2)
            for j in range(G):
                i = pe.matmul(Cb[32 * j:32 * j + 32, :], V[:, kb, g * G + j, :], Pr[:, (2 * kb + j // 2) % 4, j % 2, :],
                              start=(kb == 0), stop=(kb == TT - 1))
            i.then_inc(av, 1)

        def sums(b, g):
            pe = nc.tensor
            pe.wait_ge(osd, NG * b + g + 1)
            if g < 2:
                pe.wait_ge(mread, NG * b + 3 + g)
            else:
                pe.wait_ge(om, NG * b + g)
            for qb in range(TT):
                i = pe.matmul(Db[:, qb * G:(qb + 1) * G], oS[:, qb * P:(qb + 1) * P], selden[:, :],
                              start=True, stop=True)
            i.then_inc(den, 1)

        def spread(b, g):
            pe = nc.tensor
            pe.wait_ge(rc, NG * b + g + 1)
            for qb in range(TT):
                i = pe.transpose(Db[:, qb * P:(qb + 1) * P],
                                 recx[:, qb * P:(qb + 1) * P], ident[:, :])
            i.then_inc(rct, 1)

        def project(b, t, some):
            pe = nc.tensor
            if t == 0 and 0 in some:
                pe.wait_ge(onh, NG * b + NG - 1)
                pe.wait_ge(onl, (NG - 1) * (b + 1))
                pe.wait_ge(g_wp, 1)
                pe.wait_ge(ex, U * NG * (b + 1))
            elif t == 0:
                pe.wait_ge(onh, NG * (b + 1))
                pe.wait_ge(onl3, b + 1)
            ts = slice(t * P, (t + 1) * P)
            for g in some:
                for k, (a, c) in enumerate(((oH, WpH), (oH, WpL), (oL, WpH))):
                    i = pe.matmul(BB[t // 2][:, t % 2, 0:C], a[:, g, ts], c[:, g, :],
                                  start=(g == 0 and k == 0), stop=(g == NG - 1 and k == 2))
            return i

        def step_all(b, more):
            pe = nc.tensor
            for g in range(NG):
                for u in range(U):
                    scores(b, g, u)
                    if g < 2:
                        row_max(b, g + 2, 2 * u)
                        row_max(b, g + 2, 2 * u + 1)
                    elif more:
                        if g == 2 and u == 3:
                            pe.wait_ge(xnr[0], b + 2)
                            pe.wait_ge(mxd, N1 * NG * (b + 1))
                        if g == 2 and 3 <= u < 6:
                            t_chunk(u - 3, b + 1, t1, t1f)
                        if g == 3 and u % 2 == 0:
                            qk_tile(b + 1, u // 2)
                    if u == 0 and g in (1, 2):
                        if g == 1:
                            pe.wait_ge(mread, NG * b + 2)
                        else:
                            pe.wait_ge(om, NG * b + 1)
                        max_rows(b, g + 1)
                    if u == 2 and g == 0:
                        pe.wait_ge(mread, NG * b + 1)
                        max_rows(b, 1)
                    if u == 1 and g > 0:
                        values(b, g - 1, TT - 1)
                    if u == 3 and g > 0:
                        sums(b, g - 1)
                    if u == 5 and g > 0:
                        spread(b, g - 1)
                    if u in (3, 5, 7):
                        values(b, g, (u - 3) // 2)
            if more:
                qk_tile(b + 1, QKT - 1)
            values(b, NG - 1, TT - 1)
            if more:
                v_front(b + 1, 0)
                v_front(b + 1, 1)
            sums(b, NG - 1)
            for t in range(TT):
                project(b, t, range(NG - 1))
            spread(b, NG - 1)
            if more:
                v_front(b + 1, 2)
                v_front(b + 1, 3)
            for t in range(TT):
                i = project(b, t, (NG - 1,))
                if t % 2 == 1:
                    i.then_inc(pj, 1)
            if more:
                for n in range(PRE):
                    row_max(b + 1, 0, n)
            pe.wait_ge(xn2, TT * (b + 1))
            if more:
                pe.wait_ge(mxd, N1 * NG * (b + 1) + PRE)
            else:
                pe.wait_ge(mxd, N1 * NG * (b + 1))
            for c in range(3):
                if c == 2:
                    pe.wait_ge(xnr[1], b + 1)
                    pe.wait_ge(osd, NG * (b + 1))
                for t in range(TT):
                    i = pe.transpose((A[0], A[1], Cb)[c][:, t * P:(t + 1) * P], xs[:, t, c * P:(c + 1) * P], ident[:, :])
                i.then_inc(t2, 1)
            for m in range(FM + 2):
                units = MLP_P1[m] if m < FM and more else []
                if m < FM:
                    up(b, m, more)
                for g, n in units[:-1]:
                    row_max_mlp(b, g, n)
                if m == ROWS_AT and more:
                    pe.wait_ge(gl, 2 * FM * b + 2 * m + 1)
                    max_rows(b + 1, 0)
                if m >= 2:
                    down(b, m - 2)
                for g, n in units[-1:]:
                    row_max_mlp(b, g, n)

        def row_max_mlp(b, g, n):
            if g == 0 and PRE <= n < PRE + 2:
                nc.tensor.wait_ge(t2f, 3 * b + 2 + n - PRE)
            row_max(b + 1, g, n)

        def up(b, m, more):
            pe = nc.tensor
            if m == 0:
                pe.wait_ge(v_w1, 3)
                pe.wait_ge(g_w1, 1)
                pe.wait_ge(t2f, 3 * b + 4)
                pe.wait_ge(h2h, 2 * b + 2)
                pe.wait_ge(h2l, 2 * b + 2)
                pe.wait_ge(h2r, 2 * b + 2)
            elif m == 1:
                pe.wait_ge(om, NG * (b + 1))
            else:
                pe.wait_ge(gl, 2 * FM * b + 2 * m - 1)
            if m == ROWS_AT + 1 and more:
                pe.wait_ge(mread, NG * (b + 1) + 1)
            n = slice(m * P, (m + 1) * P)
            three(CD[m % 2][:, :],
                  [(W1H[:, k, n], W1L[:, k, n], hMH[:, k, :], hML[:, k, :]) for k in range(KC)],
                  L, (W1R[:, n], hMR[:, :])).then_inc(f1, 1)

        def down(b, m):
            pe = nc.tensor
            if m == 0:
                pe.wait_ge(pjx, 2 * (b + 1))
                pe.wait_ge(v_w2, 4)
            pe.wait_ge(gs, FM * b + m + 1)
            s = m % NG
            for t in range(TT):
                ts = slice(t * P, (t + 1) * P)
                for k, (a, c) in enumerate(((oH, W2H), (oH, W2L), (oL, W2H))):
                    i = pe.matmul(BB[t // 2][:, t % 2, 0:C], a[:, s, ts], c[:, m, :],
                                  start=(m == 0 and k == 0), stop=(m == FM - 1 and k == 2))
            i.then_inc(f2, 1)

        @block.tensor
        def _(pe):
            mm = pe.matmul
            pe.wait_ge(g_init, 5)
            pe.wait_ge(a_silu, 1)
            for k in range(3):
                i = pe.transpose(Cb[0:96, k * B:(k + 1) * B], cS[:, k * 96:(k + 1) * 96], ident[0:B, 0:B])
            i.then_inc(pe_c, 1)
            pe.wait_ge(xnr[0], 1)
            t_chunk(0, 0, t1, t1f)
            t_chunk(1, 0, t1, t1f)
            pe.wait_ge(d_bias, 16 * 4)
            pe.wait_ge(v_bias, 1)
            pe.transpose(Db[:, 0:FM + QKT], rows, ident[0:FM + QKT, 0:FM + QKT])
            for c, a in enumerate((adaR[:, 0:P], adaR[:, P:2 * P], adaX)):
                i = pe.transpose(Db[:, FM + QKT + 6 * c:FM + QKT + 6 * (c + 1)], a, ident[0:6, 0:6])
            i.then_inc(pe_bias, 1)
            pe.wait_ge(v_c, 1)
            pe.wait_ge(d_wac, 16 * 6)
            for v in range(4):
                for c in range(3):
                    o = (v * 3 + c) * B
                    if v == 0 and c == KC:
                        pe.wait_ge(v_war, 1)
                    for k in range(3):
                        i = mm(BB[0][:, 0, o:o + B], WaR[:, k, v, :] if c == KC else WaC[:, k, v, c * P:(c + 1) * P],
                               cT[:, k, :], start=(k == 0), stop=(k == 2))
            i.then_inc(pe_ada, 1)
            t_chunk(2, 0, t1, t1f)
            pe.wait_ge(d_wag, 16 * 2)
            for v in range(2):
                for k in range(3):
                    i = mm(BB[1][0:B, v, 0:C], cT[:, k, :], WaG[:, k, v, :], start=(k == 0), stop=(k == 2))
            i.then_inc(pe_gate, 1)
            for i in range(QKT):
                qk_tile(0, i)
            v_front(0, 0)
            v_front(0, 1)
            v_front(0, 2)
            v_front(0, 3)
            for n in range(N1):
                row_max(0, 0, n)
            max_rows(0, 0)
            for n in range(N1):
                row_max(0, 1, n)
            with pe.Fori(0, B - 1) as b:
                step_all(b, True)
            step_all(B - 1, False)

        def modulated(b, v, c, src, done):
            nc.scalar.activation(FT[:, c, :], src, ACT.Identity, bias=ada[:, v * 3 + c, bass.ds(b, 1)],
                                 scale=ada[:, (v + 1) * 3 + c, bass.ds(b, 1)]).then_inc(done, 1)

        def front_h(b):
            act = nc.scalar
            act.wait_ge(v_ada, 4)
            for c in range(3):
                front_hc(b, c)

        def front_hc(b, c):
            nc.scalar.wait_ge(t1, 3 * b + c + 1)
            modulated(b, 0, c, A[c % 2][:, :], t1f)

        def front_qk(b, i):
            act, m, k = nc.scalar, ORDER[i], i % QB
            n = qk_rows(m)
            act.wait_ge(qk, QKT * b + i + 1)
            if i >= QB or not (isinstance(b, int) and b == 0):
                act.wait_ge(d_scr[k], 16 * (PER[k] * b + i // QB))
            act.activation(qk3[0:n, k, 0, :], A[(i + 1) % 2][0:n, :], ACT.Identity,
                           bias=biasC[0:n, FM + m:FM + m + 1]).then_inc(qkf, 1)

        def exps(b, g, u):
            act = nc.scalar
            act.wait_ge(p2, U * (NG * b + g) + u + 1)
            if u >= 4:
                act.wait_ge(av, TT * (NG * b + g) + u // 2 - 1)
            elif g > 0:
                act.wait_ge(av, TT * (NG * b + g) + u // 2 - 1)
            act.activation(Pr[:, u % 4, :, :], BB[u % 2][:, :, :], ACT.Exp, scale=SCALE).then_inc(ex, 1)

        def take(b, g):
            act = nc.scalar
            act.wait_ge(av, TT * (NG * b + g + 1))
            if g > 0:
                act.wait_ge(onl, (NG - 1) * b + g)
            act.activation(oS[:, :], Cb[:, :], ACT.Copy).then_inc(osd, 1)

        def act_body(b, more):
            act = nc.scalar
            for g in range(NG):
                for u in range(U):
                    exps(b, g, u)
                    if u == 2 and g > 0:
                        take(b, g - 1)
                    if more:
                        if g == 2 and 3 <= u < 6:
                            front_hc(b + 1, u - 3)
                        if g == 3 and u % 2 == 0:
                            front_qk(b + 1, u // 2)
            if more:
                front_qk(b + 1, QKT - 1)
            take(b, NG - 1)
            if more:
                act.wait_ge(q3, QKT * (b + 2))
            for c in range(3):
                act.wait_ge(t2, 3 * b + c + 1)
                modulated(b, 2, c, (A[0], A[1], Cb)[c][:, :], t2f)
            for m in range(FM):
                act.wait_ge(f1, FM * b + m + 1)
                if m >= 2:
                    act.wait_ge(gs, FM * b + m - 1)
                bias = biasC[:, m:m + 1]
                act.activation(FQ[:, m % 2, :], CD[m % 2][:, :], ACT.Gelu_apprx_tanh, bias=bias).then_inc(gl, 1)
                if m == 0:
                    act.wait_ge(pj, 2 * (b + 1))
                elif m >= NG:
                    act.wait_ge(f2, FM * b + m - NG + 1)
                act.activation(oH[:, m % NG, :], CD[m % 2][:, :], ACT.Gelu_apprx_tanh, bias=bias).then_inc(gl, 1)

        @block.scalar
        def _(act):
            act.wait_ge(d_c, 16)
            act.activation(cS, cS, ACT.Silu).then_inc(a_silu, 1)
            act.wait_ge(g_init, 10)
            act.activation(seed[:, 1:2], seed[:, 0:1], ACT.Copy).then_inc(gl, 1)
            act.activation(seed[:, 2:3], seed[:, 0:1], ACT.Copy).then_inc(t2f, 1)
            front_h(0)
            for m in range(QKT):
                front_qk(0, m)
            act.wait_ge(v_w1, 3)
            act.wait_ge(g_w1, 1)
            with act.Fori(0, B - 1) as b:
                act_body(b, True)
            act_body(B - 1, False)

        def stats(b, t, src, done):
            nc.vector.bn_stats(st[:, t, :], src[:, t, 0:C]).then_inc(done, 1)

        def aggregate(b, done, step, agg):
            dve = nc.vector
            dve.wait_ge(done, TT * (b + 1))
            even, odd = 1, 4
            dve.tensor_tensor(mv[:, 0, :], st[:, :, even], st[:, :, odd], ALU.add).then_inc(step, 1)
            dve.tensor_tensor(mv[:, 1, :], st[:, :, even], st[:, :, odd], ALU.subtract).then_inc(step, 1)
            dve.tensor_tensor(mv[:, 2, :], st[:, :, even + 1], st[:, :, odd + 1], ALU.add).then_inc(step, 1)
            dve.wait_ge(step, 5 * b + 3)
            dve.tensor_scalar(mean[:, :], mv[:, 0, :], 0.5, None, ALU.mult).then_inc(step, 1)
            dve.scalar_tensor_tensor(out=mv[:, 3, :], in0=mv[:, 1, :], scalar=0.25, in1=mv[:, 1, :],
                                     op0=ALU.mult, op1=ALU.mult).then_inc(step, 1)
            dve.wait_ge(step, 5 * b + 5)
            dve.scalar_tensor_tensor(out=var[:, :], in0=mv[:, 2, :], scalar=1.0 / C, in1=mv[:, 3, :],
                                     op0=ALU.mult, op1=ALU.add).then_inc(agg, 1)

        def normed(b, w, src, ready, done):
            nc.vector.wait_ge(ready, b + 1)
            for t in range(TT):
                nc.vector.tensor_scalar(xs[:, t, 0:C], src[:, t, 0:C], mean[:, t:t + 1], rs[:, w, t:t + 1],
                                        ALU.subtract, ALU.mult).then_inc(done, 1)
            nc.vector.wait_ge(done, TT * (b + 1))
            nc.vector.tensor_copy(xs[:, :, C:3 * P].rearrange("p t (a c) -> p t a c", c=REM),
                                  xs[:, :, KC * P:C].unsqueeze(2).to_broadcast([P, TT, 3, REM])).then_inc(xnr[w], 1)

        def split_h(b, w, c):
            dve = nc.vector
            if w == 0:
                if c == 0 and not (isinstance(b, int) and b == 0):
                    dve.wait_ge(vv, TT * b)
                dve.wait_ge(t1f, 3 * b + c + 1)
            else:
                dve.wait_ge(t2f, 3 * b + c + 2)
            hh, hr, high, rest = (h1h, h1r, hAH, hAR) if w == 0 else (h2h, h2r, hMH, hMR)
            if c < KC:
                dve.tensor_copy(high[:, c, :], FT[:, c, :]).then_inc(hh, 1)
            else:
                dve.tensor_copy(rnd[:, :], FT[:, c, :]).then_inc(hr, 1)
                dve.wait_ge(hr, 2 * b + 1)
                dve.scalar_tensor_tensor(out=rest[:, :], in0=rnd[:, :].bitcast(f32), scalar=mask[:, 1:2],
                                         in1=FT[:, c, :], op0=ALU.mult, op1=ALU.add).then_inc(hr, 1)

        def second(b, i):
            dve, m, k = nc.vector, ORDER[i], i % QB
            n = qk_rows(m)
            dve.wait_ge(qkf, QKT * b + i + 1)
            if i >= 2:
                dve.wait_ge(q3, QKT * b + i - 1)
            dve.scalar_tensor_tensor(out=FQ[0:n, i % 2, :], in0=A[(i + 1) % 2][0:n, :], scalar=biasC[0:n, FM + m:FM + m + 1],
                                     in1=qk3[0:n, k, 0, :], op0=ALU.add, op1=ALU.subtract).then_inc(qr, 1)
            dve.wait_ge(qr, QKT * b + i + 1)
            dve.tensor_copy(qk3[0:n, k, 1, :], FQ[0:n, i % 2, :]).then_inc(q2, 1)

        def take_v(b, t):
            dve = nc.vector
            dve.wait_ge(vv, TT * b + t + 1)
            if t == 0:
                if isinstance(b, int) and b == 0:
                    dve.wait_ge(v_wq, 6)
                else:
                    dve.wait_ge(av, TT * NG * b)
            dve.tensor_tensor(V[:, t, :, 0:D], A[t % 2][:, 0:C].rearrange("p (h d) -> p h d", h=H),
                              biasB[:, 2, :].rearrange("p (h d) -> p h d", h=H), ALU.add).then_inc(vf, 1)

        def maximum(b, g, n):
            dve = nc.vector
            dve.wait_ge(p1, N1 * (NG * b + g) + n + 1)
            if n == 0 and not (isinstance(b, int) and b == 0 and g < 2):
                dve.wait_ge(mt, NG * b + g - 1)
            dve.tensor_reduce(mx[:, g % 2, n:n + 1], A[n % 2][:, :], AX, ALU.max, negate=True).then_inc(mxd, 1)

        def max_parts(b, g):
            dve, i, s = nc.vector, NG * b + g, g % 2
            dve.wait_ge(mt, i + 1)
            if not (isinstance(b, int) and b == 0 and g < 2):
                dve.wait_ge(d_mrow[s], 48 * (2 * b + g // 2))
            dve.tensor_copy(mr[:, s, 0, :], Db[0:N1, 0:P]).then_inc(mstep, 1)
            dve.wait_ge(mstep, 3 * i + 1)
            dve.tensor_tensor(mres[:, :], Db[0:N1, 0:P], mr[:, s, 0, :], ALU.subtract).then_inc(mread, 1)
            dve.wait_ge(mread, i + 1)
            dve.tensor_copy(mr[:, s, 1, :], mres[:, :]).then_inc(mstep, 1)
            dve.wait_ge(mstep, 3 * i + 2)
            dve.tensor_tensor(mr[:, s, 2, :], mres[:, :], mr[:, s, 1, :], ALU.subtract).then_inc(mstep, 1)

        def invert(b, g):
            nc.vector.wait_ge(den, NG * b + g + 1)
            nc.vector.reciprocal(rec[:, :], Db[:, 0:N1]).then_inc(rinv, 1)
            nc.vector.wait_ge(rinv, NG * b + g + 1)
            nc.vector.tensor_copy(recx.rearrange("p (a c) -> p a c", c=32),
                                  rec[:, :].unsqueeze(2).to_broadcast([P, N1, 32])).then_inc(rc, 1)

        def normalize(b, g):
            dve, i = nc.vector, NG * b + g + 1
            dve.wait_ge(rct, i)
            dve.tensor_tensor(oS[:, :], oS[:, :], Db[:, :], ALU.mult).then_inc(om, 1)
            dve.wait_ge(om, i)
            dve.tensor_copy(oH[:, g, :], oS[:, :]).then_inc(onh, 1)
            if g == NG - 1:
                dve.wait_ge(onh, i)
                dve.tensor_tensor(oL[:, g, :], oS[:, :], oH[:, g, :].bitcast(f32), ALU.subtract).then_inc(onl3, 1)

        def scale_add(b, ready, count, ahead, w, scaled, added, norm):
            dve = nc.vector
            for i in range(2):
                if ready is not None:
                    dve.wait_ge(ready, count + i)
                dve.tensor_tensor(BB[i][:, :, 0:C], BB[i][:, :, 0:C], gate[:, w, :].unsqueeze(1).to_broadcast([P, 2, C]),
                                  ALU.mult).then_inc(scaled, 1)
                if i == 1:
                    add_pair(b, 0, ahead, scaled, added)
            add_pair(b, 1, ahead, scaled, added)
            if norm:
                for t in range(TT):
                    dve.wait_ge(added, 2 * b + t // 2 + ahead)
                    stats(b, t, x1, ln2s)

        def add_pair(b, i, ahead, scaled, added):
            dve = nc.vector
            dve.wait_ge(scaled, 2 * b + i + 1)
            dve.tensor_tensor(x1[:, 2 * i:2 * i + 2, :], x1[:, 2 * i:2 * i + 2, :], BB[i][:, :, 0:C], ALU.add).then_inc(added, 1)

        def dve_body(b, more):
            dve = nc.vector
            for g in range(NG):
                for u in range(U):
                    if g < 2:
                        maximum(b, g + 2, 2 * u)
                        maximum(b, g + 2, 2 * u + 1)
                    if g == 0 and u == 2:
                        max_parts(b, 1)
                    if g in (1, 2) and u == 0:
                        max_parts(b, g + 1)
                    if more and g == 2 and u == 0:
                        normed(b + 1, 0, xs, g_rs1, xn1)
                    if more and g == 3 and u in (1, 3, 5, 7):
                        second(b + 1, u // 2)
                    if g > 0 and u == 3:
                        invert(b, g - 1)
                    if more and g == 2 and u == 4:
                        split_h(b + 1, 0, 0)
                        split_h(b + 1, 0, 1)
                    if g > 0 and u == 5:
                        normalize(b, g - 1)
                if more and g == 1:
                    dve.wait_ge(d_x, 16 * (b + 2))
                    for t in range(TT):
                        stats(b + 1, t, xs, ln1s)
                    aggregate(b + 1, ln1s, ln1a, ln1v)
                if more and g == 2:
                    split_h(b + 1, 0, 2)
            if more:
                second(b + 1, 4)
                take_v(b + 1, 0)
                take_v(b + 1, 1)
            invert(b, NG - 1)
            normalize(b, NG - 1)
            if more:
                take_v(b + 1, 2)
                take_v(b + 1, 3)
            dve.wait_ge(d_gate, 16 * (b + 1))
            dve.wait_ge(g_x1, b + 1)
            scale_add(b, pj, 2 * b + 1, 1, 0, pjt, pjx, True)
            aggregate(b, ln2s, ln2a, ln2v)
            if more:
                maximum(b + 1, 0, 0)
                maximum(b + 1, 0, 1)
                dve.wait_ge(t1, 3 * b + 6)
            normed(b, 1, x1, g_rs2, xn2)
            for c in range(3):
                split_h(b, 1, c)
            for m in range(FM):
                units = MLP_P1[m] if more else []
                for g, n in units[:-1]:
                    maximum(b + 1, g, n)
                if m == ROWS_AT and more:
                    max_parts(b + 1, 0)
                dve.wait_ge(gl, 2 * FM * b + 2 * m + 3)
                if m >= NG:
                    dve.wait_ge(f2, FM * b + m - NG + 1)
                dve.tensor_tensor(oL[:, m % NG, :], FQ[:, m % 2, :], oH[:, m % NG, :].bitcast(f32),
                                  ALU.subtract).then_inc(gs, 1)
                for g, n in units[-1:]:
                    maximum(b + 1, g, n)
            dve.wait_ge(f2, FM * (b + 1))
            dve.wait_ge(g_x2, b + 1)
            scale_add(b, None, None, 3, 1, yt, yd, False)

        @block.vector
        def _(dve):
            tc, tt, tsc, stt = dve.tensor_copy, dve.tensor_tensor, dve.tensor_scalar, dve.scalar_tensor_tensor
            dve.memset(FQ[0:32, :, :], 0.0).then_inc(v_init, 1)
            dve.memset(WpS, 0.0).then_inc(v_init, 1)
            dve.memset(oS[:, 0:1], 0.0).then_inc(yd, 2)
            dve.wait_ge(pe_c, 1)
            tc(cT[:, :, :], Cb[0:96, 0:3 * B].rearrange("p (k b) -> p k b", k=3)).then_inc(v_c, 1)
            dve.wait_ge(d_x, 16)
            for t in range(TT):
                stats(0, t, xs, ln1s)
            aggregate(0, ln1s, ln1a, ln1v)
            dve.wait_ge(d_bias, 16 * 4)
            tc(adaX.rearrange("p (a c) -> p a c", a=4), adaR[:, KC * P:C].unsqueeze(1).to_broadcast([6, 4, REM])).then_inc(v_bias, 1)
            normed(0, 0, xs, g_rs1, xn1)
            dve.wait_ge(d_wac, 16 * 6)
            for k in range(3):
                i = tc(WaR[:, k, :, :].rearrange("p v (a c) -> p v a c", a=4),
                       WaC[:, k, :, KC * P:C].unsqueeze(2).to_broadcast([96, 4, 4, REM]))
                if k == 2:
                    i.then_inc(v_war, 1)
            dve.wait_ge(pe_bias, 1)
            tc(biasC[:, :], Db[:, 0:BC]).then_inc(v_bias, 1)
            dve.wait_ge(d_wq, 16 * KC)
            tc(WqH[:, :, :], WqS).then_inc(v_wq, 1)
            dve.wait_ge(d_wqr, 16 * 4)
            tc(WqR[:, :], X1S[:, 0:3 * C]).then_inc(v_wq, 1)
            dve.wait_ge(v_wq, 2)
            tt(WqL[:, :, :], WqS, WqH[:, :, :].bitcast(f32), ALU.subtract).then_inc(v_wq, 1)
            dve.wait_ge(g_init, 8)
            stt(out=WqR[:, :], in0=WqR[:, :].bitcast(f32), scalar=mask[:, 0:1], in1=X1S[:, 0:3 * C],
                op0=ALU.mult, op1=ALU.add).then_inc(v_wq, 1)
            dve.wait_ge(v_bias, 2)
            dve.wait_ge(pe_ada, 1)
            for v, s in ((0, 0), (2, 3)):
                bias = biasC[:, FM + QKT:BC].rearrange("p (c s) -> p s c", s=6)[:, s:s + 2, :]
                tt(ada[:, 3 * v:3 * v + 6, :].rearrange("p (v c) b -> p v c b", v=2),
                   BB[0][:, 0, 3 * v * B:(3 * v + 6) * B].rearrange("p (v c b) -> p v c b", v=2, c=3),
                   bias.unsqueeze(3).to_broadcast([P, 2, 3, B]), ALU.add).then_inc(v_ada, 1)
            dve.wait_ge(v_ada, 2)
            for v in (1, 3):
                tsc(ada[:, 3 * v:3 * v + 3, :], ada[:, 3 * v:3 * v + 3, :], 1.0, None, ALU.add).then_inc(v_ada, 1)
            dve.wait_ge(d_wp, 16 * G)
            tc(WpH[:, :, :], WpS).then_inc(v_wp, 1)
            for c in range(3):
                split_h(0, 0, c)
            dve.wait_ge(d_w2, 16)
            tc(W2H[:, :, :], W2S).then_inc(v_w2, 1)
            for m in range(QKT):
                second(0, m)
                if m < 3:
                    dve.wait_ge(v_w2, 1)
                    k = slice(m * FM // 3, (m + 1) * FM // 3)
                    tt(W2L[:, k, :], W2S[:, k, :], W2H[:, k, :].bitcast(f32), ALU.subtract).then_inc(v_w2, 1)
            dve.memset(V[:, :, :, D:32], 0.0).then_inc(v_wq, 1)
            dve.wait_ge(v_wq, 5)
            dve.memset(V[:, :, :, D:D + 1], 1.0).then_inc(v_wq, 1)
            dve.wait_ge(pe_gate, 1)
            dve.wait_ge(d_bgate, 16 * 2)
            tt(gateS, BB[1][0:B, :, 0:C], tmp[0:B, :, :], ALU.add).then_inc(v_gate, 1)
            dve.wait_ge(d_bb, 16 * 3)
            for t in range(TT):
                take_v(0, t)
            dve.wait_ge(d_w1, 16 * 6)
            tc(W1H[:, :, :], W1S[:, 0:KC, :]).then_inc(v_w1, 1)
            tc(W1R[:, :], W1S[:, KC, :]).then_inc(v_w1, 1)
            dve.wait_ge(v_w1, 2)
            stt(out=W1R[:, :], in0=W1R[:, :].bitcast(f32), scalar=mask[:, 0:1], in1=W1S[:, KC, :],
                op0=ALU.mult, op1=ALU.add).then_inc(v_w1, 1)
            for n in range(N1):
                maximum(0, 0, n)
            max_parts(0, 0)
            for n in range(N1):
                maximum(0, 1, n)
            with dve.Fori(0, B - 1) as b:
                dve_body(b, True)
            dve_body(B - 1, False)

        def inverse_std(b, w, ready, done):
            gp = nc.gpsimd
            gp.wait_ge(ready, b + 1)
            if isinstance(b, int) and b == 0 and w == 0:
                gp.wait_ge(g_one, 1)
            gp.tensor_tensor(ve[:, :], var[:, :], epsT[:, :], ALU.add).then_inc(g_ve[w], 1)
            gp.wait_ge(g_ve[w], b + 1)
            gp.tensor_tensor(rs[:, w, :], ve[:, :], half[:, :], ALU.pow).then_inc(done, 1)

        def low_h(b, w):
            gp = nc.gpsimd
            hh, hl, high, low = (h1h, h1l, hAH, hAL) if w == 0 else (h2h, h2l, hMH, hML)
            for c in range(KC):
                gp.wait_ge(hh, KC * b + c + 1)
                gp.tensor_tensor(low[:, c, :], FT[:, c, :], high[:, c, :].bitcast(f32), ALU.subtract).then_inc(hl, 1)

        def third(b, i):
            gp, n, k = nc.gpsimd, qk_rows(ORDER[i]), i % QB
            gp.wait_ge(q2, QKT * b + i + 1)
            gp.tensor_tensor(qk3[0:n, k, 2, :], FQ[0:n, i % 2, :], qk3[0:n, k, 1, :], ALU.subtract).then_inc(q3, 1)

        def low_o(b, g):
            nc.gpsimd.wait_ge(onh, NG * b + g + 1)
            nc.gpsimd.tensor_tensor(oL[:, g, :], oS[:, :], oH[:, g, :].bitcast(f32), ALU.subtract).then_inc(onl, 1)

        def gp_body(b, more):
            gp = nc.gpsimd
            gp.wait_ge(d_gate, 16 * (b + 1))
            if isinstance(b, int) is False or b == 0:
                gp.wait_ge(d_bb, 16 * 3)
            gp.tensor_tensor(gb[:, :, :], gate[:, :, :], biasB[:, 0:2, :], ALU.mult).then_inc(g_gb, 1)
            gp.wait_ge(g_gb, b + 1)
            gp.wait_ge(d_x1, 16 * (b + 1))
            gp.tensor_tensor(x1[:, :, :], x1[:, :, :], gb[:, 0, :].unsqueeze(1).to_broadcast([P, TT, C]), ALU.add).then_inc(g_x1, 1)
            low_o(b, 0)
            if more:
                inverse_std(b + 1, 0, ln1v, g_rs1)
            if more:
                low_h(b + 1, 0)
            low_o(b, 1)
            if more:
                third(b + 1, 0)
                third(b + 1, 1)
            low_o(b, 2)
            if more:
                third(b + 1, 2)
                third(b + 1, 3)
                third(b + 1, 4)
            inverse_std(b, 1, ln2v, g_rs2)
            low_h(b, 1)
            gp.wait_ge(xn2, TT * (b + 1))
            gp.tensor_tensor(x1[:, :, :], x1[:, :, :], gb[:, 1, :].unsqueeze(1).to_broadcast([P, TT, C]), ALU.add).then_inc(g_x2, 1)

        @block.gpsimd
        def _(gp):
            gp.memset(ident[:, :], 0.0).then_inc(g_init, 1)
            gp.memset(selden[:, :], 0.0).then_inc(g_init, 1)
            gp.memset(mask[:, :], 0.0).then_inc(g_init, 1)
            gp.wait_ge(g_init, 3)
            gp.affine_select(out=ident[:, :], in_=ident[:, :], compare_op=ALU.not_equal, fill=1.0,
                             base=0, pattern=[[-1, P]], channel_multiplier=1).then_inc(g_init, 1)
            gp.affine_select(out=selden[:, :], in_=selden[:, :], compare_op=ALU.not_equal, fill=1.0,
                             base=-D, pattern=[[-32, G]], channel_multiplier=1).then_inc(g_init, 1)
            for n, (q, col) in enumerate(((slice(64, P), 0), (slice(32, 64), 1), (slice(96, P), 1))):
                gp.wait_ge(g_init, 5 + n)
                gp.memset(mask[q, col:col + 1], -1.0).then_inc(g_init, 1)
            gp.wait_ge(g_init, 8)
            gp.memset(half[:, :], -0.5).then_inc(g_init, 1)
            gp.memset(seed[:, :], 0.0).then_inc(g_init, 1)
            gp.memset(epsT[:, :], EPS).then_inc(g_init, 1)
            gp.wait_ge(g_init, 11)
            gp.memset(KS[96:P, :, :], 1.0).then_inc(g_one, 1)
            inverse_std(0, 0, ln1v, g_rs1)
            gp.wait_ge(v_wp, 1)
            gp.tensor_tensor(WpL[:, :, :], WpS, WpH[:, :, :].bitcast(f32), ALU.subtract).then_inc(g_wp, 1)
            low_h(0, 0)
            for i in range(QKT):
                third(0, i)
            gp.wait_ge(v_w1, 1)
            gp.tensor_tensor(W1L[:, :, :], W1S[:, 0:KC, :], W1H[:, :, :].bitcast(f32), ALU.subtract).then_inc(g_w1, 1)
            with gp.Fori(0, B - 1) as b:
                gp_body(b, True)
            gp_body(B - 1, False)


_INS = {"x": "x", "cond": "cond_1152", "w_qkv": "L0_cond_W_qkv", "b_qkv": "L0_cond_b_qkv", "w_proj": "L0_cond_W_proj",
        "b_proj": "L0_cond_b_proj", "w_fc1": "L0_cond_W_fc1", "b_fc1": "L0_cond_b_fc1", "w_fc2": "L0_cond_W_fc2",
        "b_fc2": "L0_cond_b_fc2", "w_ada": "L0_cond_W_ada", "b_ada": "L0_cond_b_ada"}


def kernel(**inputs):
    import numpy as _np
    import concourse.bacc as _bacc
    from concourse import mybir as _mybir
    from concourse.bass_utils import run_bass_kernel_spmd as _run

    nc = _bacc.Bacc("TRN2", target_bir_lowering=False, num_devices=1)
    arrays, args = {}, {}
    for arg, name in _INS.items():
        a = _np.ascontiguousarray(inputs[name])
        arrays[f"in_{arg}"] = a
        args[arg] = nc.dram_tensor(f"in_{arg}", a.shape, _mybir.dt.from_np(a.dtype), kind="ExternalInput").ap()
    o = nc.dram_tensor("out_0", (B, L, C), _mybir.dt.float32, kind="ExternalOutput").ap()
    build(nc, out=o, **args)
    r = _run(nc, [arrays], core_ids=[0])
    return r.results[0]["out_0"]
```

```python
import concourse.bass as bass
from concourse import mybir
from contextlib import ExitStack

B, L, C = 4, 512, 288
H = 16
D = C // H
FF = 4 * C
EPS = 1e-6
SCALE = float(D) ** -0.5
P = 128
TT = L // P
KC = C // P
REM = C - KC * P
assert 4 * REM == P
G = 4
NG = H // G
SLOTS = P // D
QKT = -(-2 * H // SLOTS)
ORDER = (0, 2, 1, 3, 4)
QB = 3
PER = [len(range(i, QKT, QB)) for i in range(QB)]
QROWS = 6 * D
MROW = QROWS
FM = FF // P
BC = FM + QKT + NG
U = 2 * TT
N1 = G * TT


def qk_rows(m):
    return min(SLOTS, 2 * H - m * SLOTS) * D


def build(nc, x, cond, w_qkv, b_qkv, w_proj, b_proj, w_fc1, b_fc1, w_fc2, b_fc2, w_ada, b_ada, out):
    f32, f32r, bf16 = mybir.dt.float32, mybir.dt.float32r, mybir.dt.bfloat16
    ALU = mybir.AluOpType
    ACT = mybir.ActivationFunctionType
    AX = mybir.AxisListType.X

    ctx = ExitStack()
    with ctx:
        def sb(name, shape, dt):
            return ctx.enter_context(nc.sbuf_tensor(name, shape, dt))

        def sem(name):
            return ctx.enter_context(nc.semaphore(name))

        WqH, WqL, WqR = sb("WqH", [P, KC, 3 * C], f32r), sb("WqL", [P, KC, 3 * C], f32r), sb("WqR", [P, 3 * C], f32r)
        W1H, W1L, W1R = sb("W1H", [P, KC, FF], f32r), sb("W1L", [P, KC, FF], f32r), sb("W1R", [P, FF], f32r)
        W2H, W2L = sb("W2H", [P, FM, C], f32r), sb("W2L", [P, FM, C], f32r)
        WpH, WpL = sb("WpH", [P, NG, C], f32r), sb("WpL", [P, NG, C], f32r)
        QS, KS = sb("QS", [P, H, L], bf16), sb("KS", [P, H, L], bf16)
        Pr = sb("Pr", [P, 4, 2, L], f32)
        V = sb("V", [P, TT, H, 32], f32)
        qk3 = sb("qk3", [P, QB, 3, L], bf16)
        FT = sb("FT", [P, 3, L], f32)
        FQ = sb("FQ", [P, 2, L], f32)
        rnd = sb("rnd", [P, L], f32r)
        hAH, hAL, hAR = sb("hAH", [P, KC, L], f32r), sb("hAL", [P, KC, L], f32r), sb("hAR", [P, L], f32r)
        hMH, hML, hMR = sb("hMH", [P, KC, L], f32r), sb("hML", [P, KC, L], f32r), sb("hMR", [P, L], f32r)
        oH, oL = sb("oH", [P, NG, L], f32r), sb("oL", [P, NG, L], f32r)
        oS = sb("oS", [P, L], f32)
        xs = sb("xs", [P, TT, 3 * P], f32)
        x1 = sb("x1", [P, TT, C], f32)
        tmp = sb("tmp", [P, 2, C], f32)
        gate = sb("gate", [P, 2, C], f32)
        gb = sb("gb", [P, 2, C], f32)
        biasB = sb("biasB", [P, 2, C], f32)
        ident = sb("ident", [P, P], f32)
        selden = sb("selden", [P, G], f32)
        mask = sb("mask", [P, 2], f32)
        biasC = sb("biasC", [P, BC], f32)
        ada = sb("ada", [P, 12, B], f32)
        st, mv, rs, minus_half = sb("st", [P, TT, 6], f32), sb("mv", [P, 4, TT], f32), sb("rs", [P, 2, TT], f32), sb("minus_half", [P, TT], f32)
        mean, var = sb("mean", [P, TT], f32), sb("var", [P, TT], f32)
        seed = sb("seed", [P, 4], f32)
        mx = sb("mx", [P, 2, N1], f32)
        rec = sb("rec", [P, N1], f32)
        mr = sb("mr", [16, 2, 3, P], bf16)
        mres = sb("mres", [16, P], f32)
        QSF = QS[:, :, :].rearrange("p a b -> p (a b)").bitcast(f32)
        KSF = KS[:, :, :].rearrange("p a b -> p (a b)").bitcast(f32)
        cS = FT[0:B, 0, 0:C]
        cT = oS[0:96, 0:96].rearrange("p (k b) -> p k b", k=3)
        rows, adaR = FQ[0:BC, 0, 0:P], FQ[:, 1, 0:3 * P]
        recx = tmp[:, :, :].rearrange("p a b -> p (a b)")[:, 0:L]
        gateS = x1[0:B, 0:2, :]
        PrF = Pr[:, :, :, :].rearrange("p a b c -> p (a b c)")
        WaC = PrF[0:96, 0:12 * C].rearrange("p (k v n) -> p k v n", k=3, v=4)
        WaG = KSF[0:96, 0:6 * C].rearrange("p (k v n) -> p k v n", k=3, v=2)
        WpS = QSF[:, 0:NG * C].rearrange("p (k n) -> p k n", k=NG)
        W2S = QSF[:, NG * C:(NG + FM) * C].rearrange("p (k n) -> p k n", k=FM)
        W1S = PrF[:, 0:3 * FF].rearrange("p (k n) -> p k n", k=3)
        bvC = biasC[:, FM + QKT:BC]
        bvX = FT[:, :, :].rearrange("p a b -> p (a b)")[:, 2 * L:3 * L].rearrange("p (g n) -> p g n", g=NG)
        WqS = V[:, :, :, :].rearrange("p a b c -> p (a b c)")[:, 0:2 * 3 * C].rearrange("p (k n) -> p k n", k=2)
        X1S = x1[:, :, :].rearrange("p a b -> p (a b)")
        adaB = X1S[:, 3 * C:4 * C]

        scr = nc.dram_tensor("qk_scratch", (3, 2 * H * D, L), bf16, kind="Internal").ap()
        gscr = nc.dram_tensor("gate_scratch", (B, 2, C), f32, kind="Internal").ap()

        A = [ctx.enter_context(nc.psum_tensor(f"A{i}", [P, L], f32)) for i in range(2)]
        BB = [ctx.enter_context(nc.psum_tensor(f"B{i}", [P, 2, L], f32)) for i in range(2)]
        Cb = ctx.enter_context(nc.psum_tensor("Cb", [P, L], f32))
        Db = ctx.enter_context(nc.psum_tensor("Db", [P, L], f32))
        CD = [Cb, Db]

        d_x, d_x1, d_gate = sem("d_x"), sem("d_x1"), sem("d_gate")
        d_c, d_bias, d_bada, d_one, d_bb, d_bgate, d_wac, d_wag, d_wq, d_wqr, d_w1, d_wp, d_w2, d_gs = (sem(n) for n in (
            "d_c", "d_bias", "d_bada", "d_one", "d_bb", "d_bgate", "d_wac", "d_wag", "d_wq", "d_wqr", "d_w1", "d_wp", "d_w2", "d_gs"))
        d_scr = [sem(f"d_scr{i}") for i in range(QB)]
        d_stk = [sem(f"d_stk{i}") for i in range(NG)]
        d_mrow = [sem(f"d_mrow{i}") for i in range(2)]
        d_out = sem("d_out")
        pe_c, pe_bias, pe_ada, pe_adat, pe_gate, pe_bv = (sem(n) for n in (
            "pe_c", "pe_bias", "pe_ada", "pe_adat", "pe_gate", "pe_bv"))
        t1, qk, vv, p1, mt, p2, av, den, rct, pj, t2, f1, f2, f2h = (sem(n) for n in (
            "t1", "qk", "vv", "p1", "mt", "p2", "av", "den", "rct", "pj", "t2", "f1", "f2", "f2h"))
        a_silu, t1f, t2f, qkf, ex, osd, gl = (sem(n) for n in ("a_silu", "t1f", "t2f", "qkf", "ex", "osd", "gl"))
        m0, t1d, t2d, t2r, h2l1 = sem("m0"), sem("t1d"), sem("t2d"), sem("t2r"), sem("h2l1")
        v_bv, v_bp = sem("v_bv"), sem("v_bp")
        a_tab = sem("a_tab")
        v_init, v_c0, v_c, v_bias, v_adar, v_ada, v_gate, v_wq, v_wp, v_w2, v_w1, v_one = (sem(n) for n in (
            "v_init", "v_c0", "v_c", "v_bias", "v_adar", "v_ada", "v_gate", "v_wq", "v_wp", "v_w2", "v_w1", "v_one"))
        ln1s, ln1v, ln2s, ln2v, xn1, xn2 = (sem(n) for n in ("ln1s", "ln1v", "ln2s", "ln2v", "xn1", "xn2"))
        h1h, h1r, h2h, h2r, qr, q2, vf, mxd, mread, mstep, rc, om, onh, onl3, pjt, pjx, gs, yt, yd = (sem(n) for n in (
            "h1h", "h1r", "h2h", "h2r", "qr", "q2", "vf", "mxd", "mread", "mstep", "rc", "om", "onh", "onl3", "pjt", "pjx",
            "gs", "yt", "yd"))
        g_init, g_rs1, g_rs2, h1l, h2l, q3, onl, g_gb, g_x1, g_x2, g_wp, g_w1, g_wq = (sem(n) for n in (
            "g_init", "g_rs1", "g_rs2", "h1l", "h2l", "q3", "onl", "g_gb", "g_x1", "g_x2", "g_wp", "g_w1", "g_wq"))
        rinv, xnr, ln1a, ln2a = sem("rinv"), [sem("xnr1"), sem("xnr2")], sem("ln1a"), sem("ln2a")

        block = ctx.enter_context(nc.Block())

        EARLY = 8
        LATE = [[(g, n) for n in range(EARLY if g == 2 else 0, N1)] for g in (2, 3)]
        LATE = LATE[0] + LATE[1]
        EVEN = LATE[3:3 + 2 * (U - 2)]
        LATE_AT = [LATE[:3]] + [EVEN[len(EVEN) * u // (U - 1):len(EVEN) * (u + 1) // (U - 1)] for u in range(U - 1)]
        LAST = LATE[3 + len(EVEN):]
        LATE_AT += [LAST[len(LAST) * u // U:len(LAST) * (u + 1) // U] for u in range(U)]

        def late_bank(g, n):
            return CD[n - EARLY - 2] if g == 2 and EARLY + 2 <= n < EARLY + 4 else None

        REST = [(g, n) for g in range(3) for n in range(EARLY if g == 2 else N1)][2:]
        MLP_P1 = [REST[len(REST) * m // FM:len(REST) * (m + 1) // FM] for m in range(FM)]
        MLP_P1 = [u[-4:] + u[:-4] for u in MLP_P1]
        ROWS_AT = 4
        assert (0, N1 - 1) in sum(MLP_P1[:ROWS_AT], []) and (2, 0) in sum(MLP_P1[ROWS_AT + 1:], [])

        def load_gate(sp, b):
            sp.dma_start(gate[:, :, :], gscr[b].partition_broadcast(P)).then_inc(d_gate, 16)

        def load_x1(sp, b):
            sp.dma_start(x1[:, :, :], x[b].rearrange("(t p) c -> p t c", p=P)).then_inc(d_x1, 16)

        def mrow(sp, b, g):
            sp.wait_ge(mstep, 3 * (NG * b + g + 1))
            for j in range(3):
                sp.dma_start(QS[MROW + j:MROW + j + 1, g * G:(g + 1) * G, :], mr[:, g % 2, j, :]).then_inc(d_mrow[g % 2], 16)

        def parts_out(sp, b, i):
            m = ORDER[i]
            sp.wait_ge(q3, QKT * b + i + 1)
            r, n = m * SLOTS * D, qk_rows(m)
            sp.dma_start(scr[:, r:r + n, :].rearrange("j r t -> r j t"), qk3[0:n, i % QB, :, :]).then_inc(d_scr[i % QB], 16)

        def tiles_there(sp, count, n):
            for k in range(min(n, QB)):
                sp.wait_ge(d_scr[k], count[k, n])

        def front(sp, b):
            snap = (lambda v: v) if isinstance(b, int) else (lambda v: sp.snap(sp.to_reg(v)))
            count = {(k, n): snap(16 * (PER[k] * b + len(range(k, n, QB)))) for n in (2, 4, 5) for k in range(min(n, QB))}
            read = [None if isinstance(b, int) and b == 0 else snap(U * (NG * (b - 1) + g + 1)) for g in range(NG)]
            for i in range(3):
                parts_out(sp, b, i)
            if isinstance(b, int):
                sp.wait_ge(pe_gate, 1)
                sp.wait_ge(pe_bv, 1)
                sp.wait_ge(g_wp, 1)
                sp.wait_ge(v_wp, 2)
                sp.wait_ge(v_w2, 4)
                sp.wait_ge(d_one, 16)
            if read[0] is not None:
                sp.wait_ge(p2, read[0])
            tiles_there(sp, count, 2)
            stacks(sp, 0, None)
            parts_out(sp, b, 3)
            parts_out(sp, b, 4)
            tiles_there(sp, count, 4)
            for g in range(1, NG):
                if g == NG - 1:
                    tiles_there(sp, count, 5)
                stacks(sp, g, read[g])

        def stacks(sp, g, read):
            q0, k0 = g * G * D, (H + g * G) * D

            def part(j, r0):
                return scr[j, r0:r0 + G * D, :].rearrange("(h r) t -> r h t", r=D)

            hs = slice(g * G, (g + 1) * G)
            if read is not None:
                sp.wait_ge(p2, read)
            for i, (j, k) in enumerate(((0, 0), (0, 1), (0, 2), (1, 0), (1, 1), (2, 0))):
                sp.dma_start(QS[i * D:(i + 1) * D, hs, :], part(j, q0)).then_inc(d_stk[g], 16)
                sp.dma_start(KS[i * D:(i + 1) * D, hs, :], part(k, k0)).then_inc(d_stk[g], 16)

        def body(sp, b, more):
            mrow(sp, b, 1)
            if more:
                sp.wait_ge(yd, 2 * b + 1)
                sp.wait_ge(t1, 3 * b + 3)
                sp.wait_ge(v_init, 2)
                sp.dma_start(xs[:, :, 0:C], x[b + 1].rearrange("(t p) c -> p t c", p=P)).then_inc(d_x, 16)
            for g in (2, 3):
                mrow(sp, b, g)
            if more:
                front(sp, b + 1)
                mrow(sp, b + 1, 0)
            for i in range(2):
                sp.wait_ge(yd, 2 * b + i + 3)
                sp.wait_ge(v_init, 2)
                sp.dma_start(out[b, i * 2 * P:(i + 1) * 2 * P, :].rearrange("(t p) c -> p t c", p=P),
                             x1[:, 2 * i:2 * i + 2, :]).then_inc(d_out, 16)
            if more:
                load_gate(sp, b + 1)
                sp.wait_ge(d_out, 16 * 2 * (b + 1))
                sp.wait_ge(v_init, 2)
                load_x1(sp, b + 1)

        @block.sync
        def _(sp):
            sp.dma_start(cS, cond).then_inc(d_c, 16)
            sp.dma_start(xs[:, :, 0:C], x[0].rearrange("(t p) c -> p t c", p=P)).then_inc(d_x, 16)
            wa = w_ada.rearrange("(k p) (s n) -> p k s n", p=96, n=C)
            for k in range(3):
                sp.dma_start(WaC[:, k, 0:2, :], wa[:, k, 0:2, :]).then_inc(d_wac, 16)
                sp.dma_start(WaC[:, k, 2:4, :], wa[:, k, 3:5, :]).then_inc(d_wac, 16)
            for v, s in enumerate((0, 1, 3, 4)):
                sp.dma_start(adaB[32 * v:32 * v + 32, :], b_ada[s * C:(s + 1) * C].partition_broadcast(32)).then_inc(d_bada, 16)
            wq = w_qkv[0:KC * P, :].rearrange("(k p) n -> p k n", p=P)
            for k in range(KC):
                sp.dma_start(WqS[:, k, :], wq[:, k, :]).then_inc(d_wq, 16)
            for q in range(4):
                sp.dma_start(X1S[q * REM:(q + 1) * REM, 0:3 * C], w_qkv[KC * P:C, :]).then_inc(d_wqr, 16)
            sp.wait_ge(v_init, 1)
            sp.dma_start(FQ[0:FM, 0, 0:P], b_fc1.rearrange("(m p) -> m p", p=P)).then_inc(d_bias, 16)
            n = (2 * C) // (SLOTS * D)
            sp.dma_start(FQ[FM:FM + n, 0, 0:SLOTS * D], b_qkv[0:n * SLOTS * D].rearrange("(m p) -> m p", m=n)).then_inc(d_bias, 16)
            sp.dma_start(FQ[FM + n:FM + n + 1, 0, 0:2 * C - n * SLOTS * D],
                         b_qkv[n * SLOTS * D:2 * C].rearrange("(o p) -> o p", o=1)).then_inc(d_bias, 16)
            sp.dma_start(FQ[FM + QKT:BC, 0, 0:P].rearrange("g (j e) -> g j e", j=G)[:, :, 0:D],
                         b_qkv[2 * C:3 * C].rearrange("(g j d) -> g j d", g=NG, j=G)).then_inc(d_bias, 16)
            for v, s in enumerate((2, 5)):
                sp.dma_start(WaG[:, :, v, :], wa[:, :, s, :]).then_inc(d_wag, 16)
            sp.wait_ge(v_one, 1)
            sp.dma_start(KS[MROW:MROW + 3, :, :].rearrange("p h (a t) -> p (h a) t", t=P),
                         mr[0:3, 0, 0, :].unsqueeze(1).to_broadcast([3, H * L // P, P])).then_inc(d_one, 16)
            sp.wait_ge(v_init, 2)
            wp = w_proj.rearrange("(g j d) n -> j d g n", g=NG, j=G)
            for j in range(G):
                sp.dma_start(WpS[32 * j:32 * j + D, :, :], wp[j]).then_inc(d_wp, 16)
            sp.dma_start(W2S, w_fc2.rearrange("(k p) n -> p k n", p=P)).then_inc(d_w2, 16)
            for i, s in enumerate((2, 5)):
                sp.dma_start(tmp[0:B, i, :], b_ada[s * C:(s + 1) * C].partition_broadcast(B)).then_inc(d_bgate, 16)
            for i, v in enumerate((b_proj[:], b_fc2[:])):
                sp.dma_start(biasB[:, i, :], v.partition_broadcast(P)).then_inc(d_bb, 16)
            sp.wait_ge(pe_ada, 1)
            w1 = w_fc1[0:KC * P, :].rearrange("(k p) n -> p k n", p=P)
            for k in range(KC):
                sp.dma_start(W1S[:, k, :], w1[:, k, :]).then_inc(d_w1, 16)
            for q in range(4):
                sp.dma_start(W1S[q * REM:(q + 1) * REM, KC, :], w_fc1[KC * P:C, :]).then_inc(d_w1, 16)
            front(sp, 0)
            sp.wait_ge(v_gate, 1)
            sp.dma_start(gscr[:, :, :], gateS).then_inc(d_gs, 16)
            sp.wait_ge(d_gs, 16)
            load_gate(sp, 0)
            mrow(sp, 0, 0)
            load_x1(sp, 0)
            with sp.Fori(0, B - 1) as b:
                body(sp, b, True)
            body(sp, B - 1, False)
            sp.wait_ge(d_out, 16 * 2 * B)

        def three(o, groups, N, tail=None):
            i, first = None, True
            for (lh, ll, rh, rl) in groups:
                for a, c in ((lh, rh), (lh, rl), (ll, rh)):
                    i = nc.tensor.matmul(o, a, c, start=first, stop=(tail is None and a is ll and lh is groups[-1][0]))
                    first = False
            if tail is not None:
                i = nc.tensor.matmul(o, tail[0], tail[1], start=False, stop=True)
            return i

        def t_chunk(c, b, done, read):
            pe = nc.tensor
            if c == 2:
                pe.wait_ge(read, 1 if isinstance(b, int) and b == 0 else 2 * b + 2)
            for t in range(TT):
                i = pe.transpose(A[c % 2][:, t * P:(t + 1) * P], xs[:, t, c * P:(c + 1) * P], ident[:, :])
            i.then_inc(done, 1)

        def qk_tile(b, i):
            pe, m = nc.tensor, ORDER[i]
            if i == 0:
                if isinstance(b, int) and b == 0:
                    pe.wait_ge(t1f, 2)
                else:
                    pe.wait_ge(t1d, b)
                pe.wait_ge(v_wq, 4)
                pe.wait_ge(g_wq, 1)
                pe.wait_ge(h1h, 2 * b + 2)
                pe.wait_ge(h1l, 2 * b + 2)
                pe.wait_ge(h1r, 2 * b + 2)
            if i == 1:
                pe.wait_ge(t1f, 2 * b + 3)
            if i >= 2:
                pe.wait_ge(qr, QKT * b + i - 1)
            r, n = m * SLOTS * D, qk_rows(m)
            three(A[(i + 1) % 2][0:n, :],
                  [(WqH[:, k, r:r + n], WqL[:, k, r:r + n], hAH[:, k, :], hAL[:, k, :]) for k in range(KC)],
                  L, (WqR[:, r:r + n], hAR[:, :])).then_inc(qk, 1)

        def v_front(b, t):
            pe = nc.tensor
            if t < 2:
                pe.wait_ge(qr, QKT * b + QKT - 1 + t)
            else:
                pe.wait_ge(vf, TT * b + t - 1)
            ts, n = slice(t * P, (t + 1) * P), slice(2 * C, 3 * C)
            three(A[t % 2][:, 0:C],
                  [(hAH[:, k, ts], hAL[:, k, ts], WqH[:, k, n], WqL[:, k, n]) for k in range(KC)],
                  C, (hAR[:, ts], WqR[:, n])).then_inc(vv, 1)

        def row_max(b, g, n, bank=None):
            pe = nc.tensor
            h, qb = g * G + n // TT, n % TT
            if n == 0:
                pe.wait_ge(d_stk[g], 192 * (b + 1))
            if bank is not None and g == 2:
                pe.wait_ge(gl, 2 * FM * b + 1)
            elif g == 2 and EARLY + 4 <= n < EARLY + 6:
                pe.wait_ge(mxd, N1 * (NG * b + g) + n - 3)
            elif n >= 2:
                pe.wait_ge(mxd, N1 * (NG * b + g) + n - 1)
            elif g == 0 and n == 0:
                pe.wait_ge(osd, NG * b)
            elif g == 0:
                pe.wait_ge(om, NG * b)
            else:
                pe.wait_ge(mxd, N1 * (NG * b + g))
            pe.matmul((A[n % 2] if bank is None else bank)[:, :], QS[0:QROWS, h, qb * P:(qb + 1) * P], KS[0:QROWS, h, :],
                      start=True, stop=True).then_inc(p1, 1)

        def row_max_pair(g, n):
            pe, i = nc.tensor, N1 * g + n
            pe.wait_ge(d_stk[g], 192)
            if i >= 4:
                pe.wait_ge(mxd, i - 2)
            for k in range(2):
                h, qb = g * G + (n + k) // TT, (n + k) % TT
                pe.matmul(BB[i // 2 % 2][:, k, :], QS[0:QROWS, h, qb * P:(qb + 1) * P], KS[0:QROWS, h, :],
                          start=True, stop=True).then_inc(p1, 1)

        def max_rows(b, g):
            nc.tensor.wait_ge(mxd, N1 * (NG * b + g + 1))
            nc.tensor.transpose(Db[0:N1, 0:P], mx[:, g % 2, :], ident[:, :]).then_inc(mt, 1)

        def scores(b, g, u):
            pe = nc.tensor
            kb, hp = u // 2, u % 2
            if u == 0:
                pe.wait_ge(d_mrow[g % 2], 48 * (2 * b + g // 2 + 1))
            if g == 0 and u < 2:
                pe.wait_ge(yd, 2 * b + u + 1)
            else:
                pe.wait_ge(ex, U * (NG * b + g) + u - 1)
            for j in range(2):
                h = g * G + 2 * hp + j
                i = pe.matmul(BB[u % 2][:, j, :], KS[0:MROW + 3, h, kb * P:(kb + 1) * P], QS[0:MROW + 3, h, :],
                              start=True, stop=True)
            i.then_inc(p2, 1)

        def values(b, g, kb):
            pe = nc.tensor
            if kb == 0:
                if g == 0:
                    pe.wait_ge(mxd, N1 * (NG * b + 2) + EARLY + 3)
                    pe.wait_ge(vf, TT * (b + 1))
                else:
                    pe.wait_ge(osd, NG * b + g)
            pe.wait_ge(ex, U * (NG * b + g) + 2 * kb + 2)
            for j in range(G):
                i = pe.matmul(Cb[32 * j:32 * j + 32, :], V[:, kb, g * G + j, :], Pr[:, (2 * kb + j // 2) % 4, j % 2, :],
                              start=(kb == 0), stop=(kb == TT - 1))
            i.then_inc(av, 1)

        def sums(b, g):
            pe = nc.tensor
            pe.wait_ge(osd, NG * b + g + 1)
            if g < 2:
                pe.wait_ge(mread, NG * b + 3 + g)
            else:
                pe.wait_ge(om, NG * b + g)
            for qb in range(TT):
                i = pe.matmul(Db[:, qb * G:(qb + 1) * G], oS[:, qb * P:(qb + 1) * P], selden[:, :],
                              start=True, stop=True)
            i.then_inc(den, 1)

        def spread(b, g):
            pe = nc.tensor
            pe.wait_ge(rc, NG * b + g + 1)
            for qb in range(TT):
                i = pe.transpose(Db[:, qb * P:(qb + 1) * P],
                                 recx[:, qb * P:(qb + 1) * P], ident[:, :])
            i.then_inc(rct, 1)

        def project(b, t, some, products=()):
            pe = nc.tensor
            if t == 0 and 0 in some:
                pe.wait_ge(onh, NG * b + NG - 1)
                pe.wait_ge(onl, (NG - 1) * (b + 1))
                pe.wait_ge(v_wp, 2)
                pe.wait_ge(g_wp, 1)
                pe.wait_ge(ex, U * NG * (b + 1))
            ts = slice(t * P, (t + 1) * P)
            for g in some:
                for k, (a, c) in enumerate(((oH, WpH), (oH, WpL), (oL, WpH))):
                    if g == NG - 1 and k not in products:
                        continue
                    i = pe.matmul(BB[t // 2][:, t % 2, 0:C], a[:, g, ts], c[:, g, :],
                                  start=(g == 0 and k == 0), stop=(g == NG - 1 and k == 2))
            return i

        def step_all(b, more):
            pe = nc.tensor
            for g in range(NG):
                for u in range(U):
                    late = LATE_AT[g * U + u] if g * U + u < 2 * U else []
                    first = 2 if (g, u) == (0, 0) else 1
                    for h, n in late[0:first]:
                        row_max(b, h, n, late_bank(h, n))
                    scores(b, g, u)
                    for h, n in late[first:]:
                        row_max(b, h, n, late_bank(h, n))
                    if g >= 2 and more:
                        if g == 2 and u == 3:
                            pe.wait_ge(xnr[0], b + 2)
                            pe.wait_ge(mxd, N1 * NG * (b + 1))
                        if g == 2 and 3 <= u < 6:
                            t_chunk(u - 3, b + 1, t1, t1f)
                        if g == 3 and u % 2 == 0:
                            qk_tile(b + 1, u // 2)
                    if (g, u) == (1, 1):
                        pe.wait_ge(mread, NG * b + 2)
                        max_rows(b, 2)
                    if (g, u) == (2, 1):
                        pe.wait_ge(om, NG * b + 1)
                        max_rows(b, 3)
                    if u == 2 and g == 0:
                        pe.wait_ge(mread, NG * b + 1)
                        pe.wait_ge(mxd, N1 * (NG * b + 2) + EARLY + 4)
                        max_rows(b, 1)
                    if u == 1 and g > 0:
                        values(b, g - 1, TT - 1)
                    if u == 4 and g > 0:
                        sums(b, g - 1)
                    if u == 6 and g > 0:
                        spread(b, g - 1)
                    if u in (3, 5, 7):
                        values(b, g, (u - 3) // 2)
            if more:
                qk_tile(b + 1, QKT - 1)
            values(b, NG - 1, TT - 1)
            if more:
                v_front(b + 1, 0)
            sums(b, NG - 1)
            def end_sums(t0):
                for products in ((0, 1), (2,)):
                    if t0 == 0:
                        if products == (2,):
                            pe.wait_ge(onl3, b + 1)
                        else:
                            pe.wait_ge(onh, NG * (b + 1))
                    for t in (t0, t0 + 1):
                        i = project(b, t, (NG - 1,), products)
                i.then_inc(pj, 1)

            project(b, 0, range(NG - 1))
            spread(b, NG - 1)
            project(b, 1, range(NG - 1))
            project(b, 2, range(NG - 1))
            end_sums(0)
            project(b, 3, range(NG - 1))
            end_sums(2)
            if more:
                v_front(b + 1, 1)
                pe.wait_ge(pjt, 2 * (b + 1))
                v_front(b + 1, 2)
                pe.wait_ge(pjx, 2 * (b + 1))
                v_front(b + 1, 3)
                pe.wait_ge(ln2s, TT * (b + 1))
                row_max(b + 1, 0, 0, Cb)
                pe.wait_ge(ln2v, b + 1)
                row_max(b + 1, 0, 1, Db)
            if more:
                pe.wait_ge(vf, TT * (b + 2))
            for t in range(TT):
                pe.wait_ge(xn2, TT * b + t + 1)
                for c in range(KC):
                    i = pe.transpose(A[c][:, t * P:(t + 1) * P], xs[:, t, c * P:(c + 1) * P], ident[:, :])
                    if t == TT - 1:
                        i.then_inc(t2, 1)
            pe.wait_ge(xnr[1], b + 1)
            pe.wait_ge(pjx, 2 * (b + 1))
            for t in range(TT):
                i = pe.transpose(BB[0][:, 0, t * P:(t + 1) * P], xs[:, t, KC * P:3 * P], ident[:, :])
            i.then_inc(t2, 1)
            for m in range(FM + 2):
                units = MLP_P1[m] if m < FM and more else []
                for g, n in units[4:]:
                    row_max_mlp(b, g, n)
                for half in range(2):
                    if m < FM:
                        up(b, m, half, more)
                    for g, n in units[half:half + 1]:
                        row_max_mlp(b, g, n)
                if m == ROWS_AT and more:
                    pe.wait_ge(gl, 2 * FM * b + 2 * m + 1)
                    max_rows(b + 1, 0)
                for half in range(2):
                    if m >= 2:
                        down(b, m - 2, half)
                    for g, n in units[2 + half:3 + half]:
                        row_max_mlp(b, g, n)

        def row_max_mlp(b, g, n):
            if g == 0 and n == 2:
                nc.tensor.wait_ge(t2f, 2 * b + 2)
            elif g == 0 and n == 3:
                nc.tensor.wait_ge(t2d, b + 1)
            row_max(b + 1, g, n)

        def up(b, m, half, more):
            pe = nc.tensor
            if half == 0 and m == 0:
                pe.wait_ge(v_w1, 3)
                pe.wait_ge(g_w1, 1)
                pe.wait_ge(osd, NG * (b + 1))
            elif half == 0 and m == 1:
                pe.wait_ge(om, NG * (b + 1))
            elif half == 0:
                pe.wait_ge(gl, 2 * FM * b + 2 * m - 1)
            if half == 0 and m < 2 and more:
                pe.wait_ge(mxd, N1 * NG * (b + 1) + m + 1)
            if half == 0 and m == ROWS_AT + 1 and more:
                pe.wait_ge(mread, NG * (b + 1) + 1)
            n = slice(m * P, (m + 1) * P)
            if half == 0:
                for k in range(KC):
                    if m == 0:
                        pe.wait_ge(h2h, 2 * b + k + 1)
                    for w in (W1H, W1L):
                        pe.matmul(CD[m % 2][:, :], w[:, k, n], hMH[:, k, :], start=(k == 0 and w is W1H), stop=False)
            else:
                for k in range(KC):
                    if m == 0:
                        pe.wait_ge((h2l, h2l1)[k], b + 1)
                    pe.matmul(CD[m % 2][:, :], W1H[:, k, n], hML[:, k, :], start=False, stop=False)
                if m == 0:
                    pe.wait_ge(h2r, b + 1)
                pe.matmul(CD[m % 2][:, :], W1R[:, n], hMR[:, :], start=False, stop=True).then_inc(f1, 1)

        def down(b, m, half):
            pe = nc.tensor
            if m == 0 and half == 0:
                pe.wait_ge(pjx, 2 * (b + 1))
                pe.wait_ge(v_w2, 4)
            if half == 0:
                pe.wait_ge(gs, FM * b + m + 1)
            s = m % NG
            for t in (2 * half, 2 * half + 1):
                ts = slice(t * P, (t + 1) * P)
                for k, (a, c) in enumerate(((oH, W2H), (oH, W2L), (oL, W2H))):
                    i = pe.matmul(BB[t // 2][:, t % 2, 0:C], a[:, s, ts], c[:, m, :],
                                  start=(m == 0 and k == 0), stop=(m == FM - 1 and k == 2))
                if m == FM - 1 and t == 1:
                    i.then_inc(f2h, 1)
            if half == 1:
                i.then_inc(f2, 1)

        @block.tensor
        def _(pe):
            mm = pe.matmul
            pe.wait_ge(g_init, 5)
            pe.wait_ge(a_silu, 1)
            for k in range(3):
                i = pe.transpose(Cb[0:96, k * B:(k + 1) * B], cS[:, k * 96:(k + 1) * 96], ident[0:B, 0:B])
            i.then_inc(pe_c, 1)
            pe.wait_ge(v_c, 1)
            pe.wait_ge(d_wac, 16 * 6)
            for k in range(3):
                for v in range(4):
                    i = mm(BB[0][32 * v:32 * v + 32, 0, 0:C], cT[:, k, :], WaC[:, k, v, :], start=(k == 0), stop=(k == 2))
            i.then_inc(pe_ada, 1)
            pe.wait_ge(xnr[0], 1)
            t_chunk(0, 0, t1, t1f)
            t_chunk(1, 0, t1, t1f)
            pe.wait_ge(v_adar, 2)
            for c in range(3):
                i = pe.transpose(Cb[:, c * P:(c + 1) * P], adaR[:, c * P:(c + 1) * P], ident[:, :])
            i.then_inc(pe_adat, 1)
            pe.wait_ge(d_bias, 16 * 4)
            pe.transpose(Db[:, 0:BC], rows, ident[0:BC, 0:BC]).then_inc(pe_bias, 1)
            t_chunk(2, 0, t1, t1f)
            pe.wait_ge(d_wag, 16 * 2)
            for v in range(2):
                for k in range(3):
                    i = mm(BB[1][0:B, v, 0:C], cT[:, k, 0:B], WaG[:, k, v, :], start=(k == 0), stop=(k == 2))
            i.then_inc(pe_gate, 1)
            for i in range(QKT):
                qk_tile(0, i)
                if i == 2:
                    pe.wait_ge(v_bv, 1)
                    for g in range(NG):
                        j = mm(BB[0][:, 1, 0:C], bvX[:, g, :], WpS[:, g, :], start=(g == 0), stop=(g == NG - 1))
                    j.then_inc(pe_bv, 1)
            v_front(0, 0)
            v_front(0, 1)
            v_front(0, 2)
            v_front(0, 3)
            pe.wait_ge(v_gate, 1)
            pe.wait_ge(v_bp, 1)
            pe.wait_ge(vf, TT)
            for n in range(0, N1, 2):
                row_max_pair(0, n)
            max_rows(0, 0)
            for g, n in [(1, n) for n in range(0, N1, 2)] + [(2, n) for n in range(0, EARLY, 2)]:
                row_max_pair(g, n)
            pe.wait_ge(mxd, 2 * N1 + EARLY)
            with pe.Fori(0, B - 1) as b:
                step_all(b, True)
            step_all(B - 1, False)

        def modulated(b, v, c, src, done):
            nc.scalar.activation(FT[:, c, :], src, ACT.Identity, bias=ada[:, v * 3 + c, bass.ds(b, 1)],
                                 scale=ada[:, (v + 1) * 3 + c, bass.ds(b, 1)]).then_inc(done, 1)

        def front_h(b):
            act = nc.scalar
            act.wait_ge(v_ada, 2)
            for c in range(3):
                front_hc(b, c)

        def front_hc(b, c):
            if c == 1 and not (isinstance(b, int) and b == 0):
                return
            nc.scalar.wait_ge(t1, 3 * b + c + 1)
            modulated(b, 0, c, A[c % 2][:, :], t1f)

        def front_qk(b, i):
            act, m, k = nc.scalar, ORDER[i], i % QB
            n = qk_rows(m)
            act.wait_ge(qk, QKT * b + i + 1)
            if i >= QB or not (isinstance(b, int) and b == 0):
                act.wait_ge(d_scr[k], 16 * (PER[k] * b + i // QB))
            act.activation(qk3[0:n, k, 0, :], A[(i + 1) % 2][0:n, :], ACT.Identity,
                           bias=biasC[0:n, FM + m:FM + m + 1]).then_inc(qkf, 1)

        def take_v(b, t):
            act = nc.scalar
            act.wait_ge(vv, TT * b + t + 1)
            if t == 0:
                if isinstance(b, int) and b == 0:
                    act.wait_ge(v_wq, 6)
                else:
                    act.wait_ge(av, TT * NG * b)
            act.activation(V[:, t, :, 0:D], A[t % 2][:, 0:C].rearrange("p (h d) -> p h d", h=H), ACT.Copy).then_inc(vf, 1)

        def exps(b, g, u):
            act = nc.scalar
            act.wait_ge(p2, U * (NG * b + g) + u + 1)
            if u >= 4:
                act.wait_ge(av, TT * (NG * b + g) + u // 2 - 1)
            elif g > 0:
                act.wait_ge(av, TT * (NG * b + g) + u // 2 - 1)
            act.activation(Pr[:, u % 4, :, :], BB[u % 2][:, :, :], ACT.Exp, scale=SCALE).then_inc(ex, 1)

        def take(b, g):
            act = nc.scalar
            act.wait_ge(av, TT * (NG * b + g + 1))
            if g > 0:
                act.wait_ge(onl, (NG - 1) * b + g)
            act.activation(oS[:, :], Cb[:, :], ACT.Copy).then_inc(osd, 1)

        def max_first(b, g):
            act, i, s = nc.scalar, NG * b + g, g % 2
            act.wait_ge(mt, i + 1)
            if not (isinstance(b, int) and b == 0 and g < 2):
                act.wait_ge(d_mrow[s], 48 * (2 * b + g // 2))
            act.activation(mr[:, s, 0, :], Db[0:N1, 0:P], ACT.Copy).then_inc(m0, 1)
            if not (isinstance(b, int) and b == 0 and g < 1):
                act.wait_ge(mstep, 3 * i)
            act.activation(mres[:, :], Db[0:N1, 0:P], ACT.Copy).then_inc(mread, 1)

        def act_body(b, more):
            act = nc.scalar
            for g in range(NG):
                for u in range(U):
                    exps(b, g, u)
                    if u == 1 and g > 0:
                        take(b, g - 1)
                    if (g, u) in ((0, 2), (1, 1), (2, 1)):
                        max_first(b, g + 1)
                    if u == 7 and g in (1, 3):
                        act.wait_ge(om, NG * b + g)
                        act.activation(oH[:, g - 1, :], oS[:, :], ACT.Copy).then_inc(onh, 1)
                    if more:
                        if g == 2 and 3 <= u < 6:
                            front_hc(b + 1, u - 3)
                        if g == 3 and u % 2 == 0:
                            front_qk(b + 1, u // 2)
            if more:
                front_qk(b + 1, QKT - 1)
            take(b, NG - 1)
            if more:
                for t in range(TT):
                    take_v(b + 1, t)
                act.wait_ge(q3, QKT * (b + 2))
            for c, bank in ((0, A[0][:, :]), (2, BB[0][:, 0, :])):
                act.wait_ge(t2, 3 * b + c + 1)
                modulated(b, 2, c, bank, t2f)
            act.activation(rnd[:, :], BB[0][:, 0, :], ACT.Identity, bias=ada[:, 8, bass.ds(b, 1)],
                           scale=ada[:, 11, bass.ds(b, 1)]).then_inc(t2r, 1)
            for m in range(FM):
                act.wait_ge(f1, FM * b + m + 1)
                if m >= 2:
                    act.wait_ge(gs, FM * b + m - 1)
                bias = biasC[:, m:m + 1]
                act.activation(FQ[:, m % 2, :], CD[m % 2][:, :], ACT.Gelu_apprx_tanh, bias=bias).then_inc(gl, 1)
                if m == 0:
                    act.wait_ge(pj, 2 * (b + 1))
                elif m >= NG:
                    act.wait_ge(f2, FM * b + m - NG + 1)
                act.activation(oH[:, m % NG, :], CD[m % 2][:, :], ACT.Gelu_apprx_tanh, bias=bias).then_inc(gl, 1)
                if m == ROWS_AT and more:
                    max_first(b + 1, 0)
            act.activation(seed[:, 3:4], seed[:, 0:1], ACT.Exp).then_inc(a_tab, 1)

        @block.scalar
        def _(act):
            act.wait_ge(d_c, 16)
            act.activation(cS, cS, ACT.Silu).then_inc(a_silu, 1)
            act.wait_ge(g_init, 10)
            act.activation(seed[:, 1:2], seed[:, 0:1], ACT.Copy).then_inc(gl, 1)
            act.activation(seed[:, 2:3], seed[:, 0:1], ACT.Copy).then_inc(t2f, 1)
            front_h(0)
            for m in range(QKT):
                front_qk(0, m)
            for t in range(TT):
                take_v(0, t)
            act.wait_ge(v_w1, 3)
            act.wait_ge(g_w1, 1)
            max_first(0, 0)
            with act.Fori(0, B - 1) as b:
                act_body(b, True)
            act_body(B - 1, False)

        def stats(b, t, src, done):
            nc.vector.bn_stats(st[:, t, :], src[:, t, 0:C]).then_inc(done, 1)

        def aggregate(b, done, step, agg):
            dve = nc.vector
            dve.wait_ge(done, TT * (b + 1))
            even, odd = 1, 4
            dve.tensor_tensor(mv[:, 0, :], st[:, :, even], st[:, :, odd], ALU.add).then_inc(step, 1)
            dve.tensor_tensor(mv[:, 1, :], st[:, :, even], st[:, :, odd], ALU.subtract).then_inc(step, 1)
            dve.scalar_tensor_tensor(out=mv[:, 2, :], in0=st[:, :, even + 1], scalar=C * EPS, in1=st[:, :, odd + 1],
                                     op0=ALU.add, op1=ALU.add).then_inc(step, 1)
            dve.wait_ge(step, 5 * b + 3)
            dve.tensor_scalar(mean[:, :], mv[:, 0, :], 0.5, None, ALU.mult).then_inc(step, 1)
            dve.scalar_tensor_tensor(out=mv[:, 3, :], in0=mv[:, 1, :], scalar=0.25, in1=mv[:, 1, :],
                                     op0=ALU.mult, op1=ALU.mult).then_inc(step, 1)
            dve.wait_ge(step, 5 * b + 5)
            dve.scalar_tensor_tensor(out=var[:, :], in0=mv[:, 2, :], scalar=1.0 / C, in1=mv[:, 3, :],
                                     op0=ALU.mult, op1=ALU.add).then_inc(agg, 1)

        def normed(b, w, src, ready, done):
            nc.vector.wait_ge(ready, b + 1)
            for t in range(TT):
                nc.vector.tensor_scalar(xs[:, t, 0:C], src[:, t, 0:C], mean[:, t:t + 1], rs[:, w, t:t + 1],
                                        ALU.subtract, ALU.mult).then_inc(done, 1)
            nc.vector.wait_ge(done, TT * (b + 1))
            nc.vector.tensor_copy(xs[:, :, C:3 * P].rearrange("p t (a c) -> p t a c", c=REM),
                                  xs[:, :, KC * P:C].unsqueeze(2).to_broadcast([P, TT, 3, REM])).then_inc(xnr[w], 1)

        def split_h(b, w, c):
            dve = nc.vector
            hh, hr, high, rest = (h1h, h1r, hAH, hAR) if w == 0 else (h2h, h2r, hMH, hMR)
            if w == 0:
                if c == 0 and not (isinstance(b, int) and b == 0):
                    dve.wait_ge(vv, TT * b)
                if isinstance(b, int) and b == 0:
                    dve.wait_ge(t1f, c + 1)
                elif c == 1:
                    dve.wait_ge(t1d, b)
                else:
                    dve.wait_ge(t1f, 2 * b + c // 2 + 2)
            elif c == 1:
                dve.wait_ge(t2d, b + 1)
            else:
                dve.wait_ge(t2f, 2 * b + c // 2 + 2)
            if c < KC:
                dve.tensor_copy(high[:, c, :], FT[:, c, :]).then_inc(hh, 1)
                return
            if w == 0:
                dve.tensor_copy(rnd[:, :], FT[:, c, :]).then_inc(hr, 1)
                dve.wait_ge(hr, 2 * b + 1)
            else:
                dve.wait_ge(t2r, b + 1)
            dve.scalar_tensor_tensor(out=rest[:, :], in0=rnd[:, :].bitcast(f32), scalar=mask[:, 1:2],
                                     in1=FT[:, c, :], op0=ALU.mult, op1=ALU.add).then_inc(hr, 1)

        def second(b, i):
            dve, m, k = nc.vector, ORDER[i], i % QB
            n = qk_rows(m)
            dve.wait_ge(qkf, QKT * b + i + 1)
            if i >= 2:
                dve.wait_ge(q3, QKT * b + i - 1)
            dve.scalar_tensor_tensor(out=FQ[0:n, i % 2, :], in0=A[(i + 1) % 2][0:n, :], scalar=biasC[0:n, FM + m:FM + m + 1],
                                     in1=qk3[0:n, k, 0, :], op0=ALU.add, op1=ALU.subtract).then_inc(qr, 1)
            dve.wait_ge(qr, QKT * b + i + 1)
            dve.tensor_copy(qk3[0:n, k, 1, :], FQ[0:n, i % 2, :]).then_inc(q2, 1)

        def maximum(b, g, n, bank=None):
            dve = nc.vector
            dve.wait_ge(p1, N1 * (NG * b + g) + n + 1)
            if n == 0 and not (isinstance(b, int) and b == 0 and g < 2):
                dve.wait_ge(mt, NG * b + g - 1)
            dve.tensor_reduce(mx[:, g % 2, n:n + 1], (A[n % 2] if bank is None else bank)[:, :], AX, ALU.max, negate=True).then_inc(mxd, 1)

        def maximum_pair(g, n):
            dve, i = nc.vector, N1 * g + n
            dve.wait_ge(p1, i + 2)
            if g == 2 and n == 0:
                dve.wait_ge(mt, 1)
            dve.tensor_reduce(mx[:, g % 2, n:n + 2], BB[i // 2 % 2][:, :, :], AX, ALU.max, negate=True).then_inc(mxd, 2)

        def invert(b, g):
            nc.vector.wait_ge(den, NG * b + g + 1)
            nc.vector.reciprocal(rec[:, :], Db[:, 0:N1]).then_inc(rinv, 1)
            nc.vector.wait_ge(rinv, NG * b + g + 1)
            nc.vector.tensor_copy(recx.rearrange("p (a c) -> p a c", c=32),
                                  rec[:, :].unsqueeze(2).to_broadcast([P, N1, 32])).then_inc(rc, 1)

        def normalize(b, g):
            dve, i = nc.vector, NG * b + g + 1
            dve.wait_ge(rct, i)
            dve.tensor_tensor(oS[:, :], oS[:, :], Db[:, :], ALU.mult).then_inc(om, 1)
            if g in (1, 3):
                dve.wait_ge(om, i)
                dve.tensor_copy(oH[:, g, :], oS[:, :]).then_inc(onh, 1)
            if g == NG - 1:
                dve.wait_ge(onh, i)
                dve.tensor_tensor(oL[:, g, :], oS[:, :], oH[:, g, :].bitcast(f32), ALU.subtract).then_inc(onl3, 1)

        def scale_add(b, ahead, w, scaled, added, norm):
            dve = nc.vector
            for i in range(2):
                if norm:
                    dve.wait_ge(pj, 2 * b + i + 1)
                elif i == 0:
                    dve.wait_ge(f2h, b + 1)
                else:
                    dve.wait_ge(f2, FM * (b + 1))
                dve.tensor_tensor(BB[i][:, :, 0:C], BB[i][:, :, 0:C], gate[:, w, :].unsqueeze(1).to_broadcast([P, 2, C]),
                                  ALU.mult).then_inc(scaled, 1)
                add_pair(b, i, ahead, scaled, added)
                if norm:
                    dve.wait_ge(added, 2 * b + i + 1)
                    for t in (2 * i, 2 * i + 1):
                        stats(b, t, x1, ln2s)

        def add_pair(b, i, ahead, scaled, added):
            dve = nc.vector
            dve.wait_ge(scaled, 2 * b + i + 1)
            dve.tensor_tensor(x1[:, 2 * i:2 * i + 2, :], x1[:, 2 * i:2 * i + 2, :], BB[i][:, :, 0:C], ALU.add).then_inc(added, 1)

        def dve_body(b, more):
            dve = nc.vector
            for g in range(NG):
                for u in range(U):
                    if g * U + u < 2 * U:
                        for h, n in LATE_AT[g * U + u]:
                            maximum(b, h, n, late_bank(h, n))
                    if more and g == 2 and u == 0:
                        normed(b + 1, 0, xs, g_rs1, xn1)
                    if more and g == 1 and u == 4:
                        dve.wait_ge(d_x, 16 * (b + 2))
                        for t in range(TT):
                            stats(b + 1, t, xs, ln1s)
                    if more and g == 1 and u == 5:
                        aggregate(b + 1, ln1s, ln1a, ln1v)
                    if more and g == 3 and u in (1, 3, 5, 7):
                        second(b + 1, u // 2)
                    if g > 0 and u == 4:
                        invert(b, g - 1)
                    if more and g == 2 and u == 4:
                        split_h(b + 1, 0, 0)
                        dve.wait_ge(t1, 3 * b + 5)
                        dve.tensor_scalar(FT[:, 1, :], A[1][:, :], ada[:, 4, bass.ds(b + 1, 1)], ada[:, 1, bass.ds(b + 1, 1)],
                                          ALU.mult, ALU.add).then_inc(t1d, 1)
                        split_h(b + 1, 0, 1)
                    if more and g == 2 and u == 6:
                        split_h(b + 1, 0, 2)
                    if g > 0 and u == 6:
                        normalize(b, g - 1)
            if more:
                second(b + 1, 4)
            invert(b, NG - 1)
            normalize(b, NG - 1)
            dve.wait_ge(d_gate, 16 * (b + 1))
            dve.wait_ge(g_x1, b + 1)
            scale_add(b, 1, 0, pjt, pjx, True)
            aggregate(b, ln2s, ln2a, ln2v)
            if more:
                maximum(b + 1, 0, 0, Cb)
                maximum(b + 1, 0, 1, Db)
                dve.wait_ge(t1, 3 * b + 6)
            normed(b, 1, x1, g_rs2, xn2)
            dve.wait_ge(t2, 3 * b + 2)
            dve.tensor_scalar(FT[:, 1, :], A[1][:, :], ada[:, 10, bass.ds(b, 1)], ada[:, 7, bass.ds(b, 1)],
                              ALU.mult, ALU.add).then_inc(t2d, 1)
            split_h(b, 1, 0)
            split_h(b, 1, 1)
            dve.wait_ge(h2h, 2 * b + 2)
            dve.tensor_tensor(hML[:, 1, :], FT[:, 1, :], hMH[:, 1, :].bitcast(f32), ALU.subtract).then_inc(h2l1, 1)
            split_h(b, 1, 2)
            for m in range(FM):
                units = MLP_P1[m] if more else []
                for g, n in units[4:] + units[0:2]:
                    maximum(b + 1, g, n)
                for g, n in units[2:3]:
                    maximum(b + 1, g, n)
                dve.wait_ge(gl, 2 * FM * b + 2 * m + 3)
                if m >= NG:
                    dve.wait_ge(f2, FM * b + m - NG + 1)
                dve.tensor_tensor(oL[:, m % NG, :], FQ[:, m % 2, :], oH[:, m % NG, :].bitcast(f32),
                                  ALU.subtract).then_inc(gs, 1)
                for g, n in units[3:4]:
                    maximum(b + 1, g, n)
            dve.wait_ge(g_x2, b + 1)
            scale_add(b, 3, 1, yt, yd, False)

        @block.vector
        def _(dve):
            tc, tt, tsc, stt = dve.tensor_copy, dve.tensor_tensor, dve.tensor_scalar, dve.scalar_tensor_tensor
            dve.memset(FQ[0:32, 0, 0:P], 0.0).then_inc(v_init, 1)
            dve.memset(cT[:, :, :], 0.0).then_inc(v_c0, 1)
            dve.memset(mr[0:3, 0, 0, :], 1.0).then_inc(v_one, 1)
            dve.memset(oS[:, L - 1:L], 0.0).then_inc(yd, 2)
            dve.wait_ge(pe_c, 1)
            dve.wait_ge(v_c0, 1)
            tc(cT[:, :, 0:B], Cb[0:96, 0:3 * B].rearrange("p (k b) -> p k b", k=3)).then_inc(v_c, 1)
            dve.memset(WpS, 0.0).then_inc(v_init, 1)
            dve.wait_ge(d_x, 16)
            for t in range(TT):
                stats(0, t, xs, ln1s)
            aggregate(0, ln1s, ln1a, ln1v)
            normed(0, 0, xs, g_rs1, xn1)
            dve.wait_ge(d_bada, 16 * 4)
            dve.wait_ge(pe_ada, 1)
            tt(adaR[:, 0:C], BB[0][:, 0, 0:C], adaB, ALU.add).then_inc(v_adar, 1)
            dve.wait_ge(v_adar, 1)
            tc(adaR[:, C:3 * P].rearrange("p (a c) -> p a c", c=REM),
               adaR[:, KC * P:C].unsqueeze(1).to_broadcast([P, 3, REM])).then_inc(v_adar, 1)
            dve.wait_ge(d_wq, 16 * KC)
            tc(WqH[:, :, :], WqS).then_inc(v_wq, 1)
            dve.wait_ge(d_wqr, 16 * 4)
            tc(WqR[:, :], X1S[:, 0:3 * C]).then_inc(v_wq, 1)
            dve.wait_ge(pe_adat, 1)
            for s in range(2):
                to = ada[:, :, :].rearrange("p (v s c) b -> p v s c b", v=2, s=2)[:, :, s, :, :]
                frm = Cb[:, 0:3 * P].rearrange("p (c v s x) -> p v s c x", c=3, v=2, s=2)[:, :, s, :, 0:B]
                if s == 0:
                    tc(to, frm).then_inc(v_ada, 1)
                else:
                    tsc(to, frm, 1.0, None, ALU.add).then_inc(v_ada, 1)
            dve.wait_ge(pe_bias, 1)
            tc(biasC[:, :], Db[:, 0:BC]).then_inc(v_bias, 1)
            dve.wait_ge(v_wq, 2)
            tt(WqL[:, 0, :], WqS[:, 0, :], WqH[:, 0, :].bitcast(f32), ALU.subtract).then_inc(v_wq, 1)
            split_h(0, 0, 0)
            split_h(0, 0, 1)
            dve.wait_ge(g_init, 8)
            stt(out=WqR[:, :], in0=WqR[:, :].bitcast(f32), scalar=mask[:, 0:1], in1=X1S[:, 0:3 * C],
                op0=ALU.mult, op1=ALU.add).then_inc(v_wq, 1)
            split_h(0, 0, 2)
            dve.wait_ge(d_wp, 16 * G)
            tc(WpH[:, :, :], WpS).then_inc(v_wp, 1)
            dve.wait_ge(v_wp, 1)
            tt(WpL[:, 2:4, :], WpS[:, 2:4, :], WpH[:, 2:4, :].bitcast(f32), ALU.subtract).then_inc(v_wp, 1)
            dve.wait_ge(v_bias, 1)
            dve.wait_ge(h1r, 2)
            tc(bvX, bvC.unsqueeze(2).to_broadcast([P, NG, P])).then_inc(v_bv, 1)
            dve.wait_ge(d_w2, 16)
            tc(W2H[:, :, :], W2S).then_inc(v_w2, 1)
            for m in range(QKT):
                second(0, m)
                if m < 3:
                    dve.wait_ge(v_w2, 1)
                    k = slice(m * FM // 3, (m + 1) * FM // 3)
                    tt(W2L[:, k, :], W2S[:, k, :], W2H[:, k, :].bitcast(f32), ALU.subtract).then_inc(v_w2, 1)
                if m == 2:
                    dve.wait_ge(d_w1, 16 * 6)
                    tc(W1H[:, :, :], W1S[:, 0:KC, :]).then_inc(v_w1, 1)
                    tc(W1R[:, :], W1S[:, KC, :]).then_inc(v_w1, 1)
                    dve.wait_ge(v_w1, 2)
                    stt(out=W1R[:, :], in0=W1R[:, :].bitcast(f32), scalar=mask[:, 0:1], in1=W1S[:, KC, :],
                        op0=ALU.mult, op1=ALU.add).then_inc(v_w1, 1)
            dve.memset(V[:, :, :, D:32], 0.0).then_inc(v_wq, 1)
            dve.wait_ge(v_wq, 5)
            dve.memset(V[:, :, :, D:D + 1], 1.0).then_inc(v_wq, 1)
            dve.wait_ge(pe_gate, 1)
            dve.wait_ge(d_bgate, 16 * 2)
            tt(gateS, BB[1][0:B, :, 0:C], tmp[0:B, :, :], ALU.add).then_inc(v_gate, 1)
            dve.wait_ge(d_bb, 16 * 2)
            dve.wait_ge(pe_bv, 1)
            tt(biasB[:, 0, :], biasB[:, 0, :], BB[0][:, 1, 0:C], ALU.add).then_inc(v_bp, 1)
            for n in range(0, N1, 2):
                maximum_pair(0, n)
            for n in range(0, N1, 2):
                maximum_pair(1, n)
            for n in range(0, EARLY, 2):
                maximum_pair(2, n)
            with dve.Fori(0, B - 1) as b:
                dve_body(b, True)
            dve_body(B - 1, False)

        def inverse_std(b, w, ready, done):
            gp = nc.gpsimd
            gp.wait_ge(ready, b + 1)
            if isinstance(b, int) and b == 0 and w == 0:
                gp.wait_ge(g_init, 10)
            gp.tensor_tensor(rs[:, w, :], var[:, :], minus_half[:, :], ALU.pow).then_inc(done, 1)

        def low_h(b, w):
            gp = nc.gpsimd
            hh, hl, high, low = (h1h, h1l, hAH, hAL) if w == 0 else (h2h, h2l, hMH, hML)
            for c in range(KC if w == 0 else 1):
                gp.wait_ge(hh, KC * b + c + 1)
                gp.tensor_tensor(low[:, c, :], FT[:, c, :], high[:, c, :].bitcast(f32), ALU.subtract).then_inc(hl, 1)

        def third(b, i):
            gp, n, k = nc.gpsimd, qk_rows(ORDER[i]), i % QB
            gp.wait_ge(q2, QKT * b + i + 1)
            gp.tensor_tensor(qk3[0:n, k, 2, :], FQ[0:n, i % 2, :], qk3[0:n, k, 1, :], ALU.subtract).then_inc(q3, 1)

        def low_o(b, g):
            nc.gpsimd.wait_ge(onh, NG * b + g + 1)
            nc.gpsimd.tensor_tensor(oL[:, g, :], oS[:, :], oH[:, g, :].bitcast(f32), ALU.subtract).then_inc(onl, 1)

        def max_rest(b, g):
            gp, i, s = nc.gpsimd, NG * b + g, g % 2
            gp.wait_ge(m0, i + 1)
            gp.wait_ge(mread, i + 1)
            gp.tensor_tensor(mres[:, :], mres[:, :], mr[:, s, 0, :], ALU.subtract).then_inc(mstep, 1)
            gp.wait_ge(mstep, 3 * i + 1)
            gp.tensor_tensor(mr[:, s, 1, :], mres[:, :], seed[0:16, 0:1].to_broadcast([16, P]), ALU.add).then_inc(mstep, 1)
            gp.wait_ge(mstep, 3 * i + 2)
            gp.tensor_tensor(mr[:, s, 2, :], mres[:, :], mr[:, s, 1, :], ALU.subtract).then_inc(mstep, 1)

        def gp_body(b, more):
            gp = nc.gpsimd
            max_rest(b, 1)
            gp.wait_ge(d_gate, 16 * (b + 1))
            if isinstance(b, int) is False or b == 0:
                gp.wait_ge(v_bp, 1)
            gp.tensor_tensor(gb[:, :, :], gate[:, :, :], biasB[:, 0:2, :], ALU.mult).then_inc(g_gb, 1)
            gp.wait_ge(g_gb, b + 1)
            gp.wait_ge(d_x1, 16 * (b + 1))
            gp.tensor_tensor(x1[:, :, :], x1[:, :, :], gb[:, 0, :].unsqueeze(1).to_broadcast([P, TT, C]), ALU.add).then_inc(g_x1, 1)
            max_rest(b, 2)
            if more:
                inverse_std(b + 1, 0, ln1v, g_rs1)
            low_o(b, 0)
            max_rest(b, 3)
            if more:
                low_h(b + 1, 0)
            low_o(b, 1)
            if more:
                third(b + 1, 0)
                third(b + 1, 1)
            low_o(b, 2)
            if more:
                third(b + 1, 2)
                third(b + 1, 3)
                third(b + 1, 4)
            inverse_std(b, 1, ln2v, g_rs2)
            low_h(b, 1)
            gp.wait_ge(xn2, TT * (b + 1))
            gp.tensor_tensor(x1[:, :, :], x1[:, :, :], gb[:, 1, :].unsqueeze(1).to_broadcast([P, TT, C]), ALU.add).then_inc(g_x2, 1)
            if more:
                max_rest(b + 1, 0)

        @block.gpsimd
        def _(gp):
            gp.memset(ident[:, :], 0.0).then_inc(g_init, 1)
            gp.memset(selden[:, :], 0.0).then_inc(g_init, 1)
            gp.memset(mask[:, :], 0.0).then_inc(g_init, 1)
            gp.wait_ge(g_init, 3)
            gp.affine_select(out=ident[:, :], in_=ident[:, :], compare_op=ALU.not_equal, fill=1.0,
                             base=0, pattern=[[-1, P]], channel_multiplier=1).then_inc(g_init, 1)
            gp.affine_select(out=selden[:, :], in_=selden[:, :], compare_op=ALU.not_equal, fill=1.0,
                             base=-D, pattern=[[-32, G]], channel_multiplier=1).then_inc(g_init, 1)
            for n, (q, col) in enumerate(((slice(64, P), 0), (slice(32, 64), 1), (slice(96, P), 1))):
                gp.wait_ge(g_init, 5 + n)
                gp.memset(mask[q, col:col + 1], -1.0).then_inc(g_init, 1)
            gp.wait_ge(g_init, 8)
            gp.memset(minus_half[:, :], -0.5).then_inc(g_init, 1)
            gp.memset(seed[:, :], 0.0).then_inc(g_init, 1)
            inverse_std(0, 0, ln1v, g_rs1)
            gp.wait_ge(v_wq, 1)
            gp.tensor_tensor(WqL[:, 1, :], WqS[:, 1, :], WqH[:, 1, :].bitcast(f32), ALU.subtract).then_inc(g_wq, 1)
            low_h(0, 0)
            gp.wait_ge(v_wp, 1)
            gp.tensor_tensor(WpL[:, 0:2, :], WpS[:, 0:2, :], WpH[:, 0:2, :].bitcast(f32), ALU.subtract).then_inc(g_wp, 1)
            for i in range(QKT):
                third(0, i)
            gp.wait_ge(v_w1, 1)
            gp.tensor_tensor(W1L[:, :, :], W1S[:, 0:KC, :], W1H[:, :, :].bitcast(f32), ALU.subtract).then_inc(g_w1, 1)
            max_rest(0, 0)
            with gp.Fori(0, B - 1) as b:
                gp_body(b, True)
            gp_body(B - 1, False)


_INS = {"x": "x", "cond": "cond_1152", "w_qkv": "L0_cond_W_qkv", "b_qkv": "L0_cond_b_qkv", "w_proj": "L0_cond_W_proj",
        "b_proj": "L0_cond_b_proj", "w_fc1": "L0_cond_W_fc1", "b_fc1": "L0_cond_b_fc1", "w_fc2": "L0_cond_W_fc2",
        "b_fc2": "L0_cond_b_fc2", "w_ada": "L0_cond_W_ada", "b_ada": "L0_cond_b_ada"}


def kernel(**inputs):
    import numpy as _np
    import concourse.bacc as _bacc
    from concourse import mybir as _mybir
    from concourse.bass_utils import run_bass_kernel_spmd as _run

    nc = _bacc.Bacc("TRN2", target_bir_lowering=False, num_devices=1)
    arrays, args = {}, {}
    for arg, name in _INS.items():
        a = _np.ascontiguousarray(inputs[name])
        arrays[f"in_{arg}"] = a
        args[arg] = nc.dram_tensor(f"in_{arg}", a.shape, _mybir.dt.from_np(a.dtype), kind="ExternalInput").ap()
    o = nc.dram_tensor("out_0", (B, L, C), _mybir.dt.float32, kind="ExternalOutput").ap()
    build(nc, out=o, **args)
    r = _run(nc, [arrays], core_ids=[0])
    return r.results[0]["out_0"]
```
